# Optimizing a Trainium2 kernel written in Bass

```python
import numpy as np
import jax
import jax.numpy as jnp

def _softmax(x, axis=-1):
    return jax.nn.softmax(x, axis=axis)

def _gelu(x):
    return jax.nn.gelu(x, approximate=True)

def _silu(x):
    return jax.nn.silu(x)

def _sigmoid(x):
    return jax.nn.sigmoid(x)

def _layernorm(x, axis=-1, eps=1e-05):
    m = jnp.mean(x, axis=axis, keepdims=True)
    v = jnp.var(x, axis=axis, keepdims=True)
    return (x - m) / jnp.sqrt(v + eps)

def _scatter_add(tgt, idx, src, axis=0):
    return tgt.at[idx].add(src)

def _segment_sum(src, seg, n):
    return jax.ops.segment_sum(src, seg, n)
kernel_name = 'mk_xattn_ffn_d2_seqx_r4_c0152f'

def setup_inputs(seed: int=0):
    np.random.seed(seed)
    _w = jnp.asarray

    def _rec_inputs():
        import jax
        import jax.numpy as jnp
        _rk = jax.random.key(seed)
        x = 7.22e-05 + 1 * jax.random.normal(jax.random.fold_in(_rk, 1), (32, 128, 1024), jnp.float32)
        _lenS = 128 - jax.random.randint(jax.random.fold_in(_rk, 7), (32,), 0, max(1, 128 // 4) + 1, jnp.int32)
        _lenS2 = 128 - jax.random.randint(jax.random.fold_in(_rk, 8), (32,), 0, max(1, 128 // 4) + 1, jnp.int32)
        _ctx_4096P = jax.random.normal(jax.random.fold_in(_rk, 11), (32, 16, 1024), jnp.float32)
        _ctx_4096c = jax.random.dirichlet(jax.random.fold_in(_rk, 511), 0.3 * jnp.ones((16,), jnp.float32), (32, 128))
        _ctx_4096t = jnp.einsum('bsk,bkd->bsd', _ctx_4096c, _ctx_4096P)
        _ctx_4096t = _ctx_4096t * jax.lax.rsqrt(jnp.mean(jnp.square(_ctx_4096t)) + 1e-12) * 0.953939
        ctx_4096 = 4.13588e-05 + 0.999923 * (_ctx_4096t + 0.3 * jax.random.normal(jax.random.fold_in(_rk, 611), (32, 128, 1024), jnp.float32))
        return (x, ctx_4096)
    x, ctx_4096 = _rec_inputs()

    def _L0_xattn_setup():
        import jax, jax.numpy as jnp
        import numpy as np
        B, C, T = (4, 128, 1024)
        DQK = 64
        key = jax.random.key(seed)
        ks = jax.random.split(key, 8)
        s = 1.0 / np.sqrt(C)
        return {'x': jax.random.normal(ks[0], (B, C, T), dtype=jnp.float32), 'init': jax.random.normal(ks[1], (B, C, T), dtype=jnp.float32), 'Wq': jax.random.normal(ks[2], (DQK, C), dtype=jnp.float32) * s, 'bq': jax.random.normal(ks[3], (DQK,), dtype=jnp.float32) * s, 'Wk': jax.random.normal(ks[4], (DQK, C), dtype=jnp.float32) * s, 'bk': jax.random.normal(ks[5], (DQK,), dtype=jnp.float32) * s, 'Wv': jax.random.normal(ks[6], (C, C), dtype=jnp.float32) * s, 'bv': jax.random.normal(ks[7], (C,), dtype=jnp.float32) * s}
    _L0_xattn_all = _L0_xattn_setup()
    _L0_xattn_in = {k: v for k, v in _L0_xattn_all.items() if k in ('Wq', 'bq', 'Wk', 'bk', 'Wv', 'bv')}
    del _L0_xattn_all

    def _L0_ffn_setup():
        import jax, jax.numpy as jnp
        import numpy as np

        @jax.custom_vjp
        def ste_sign(w):
            return jnp.sign(w)

        def _ste_fwd(w):
            return (jnp.sign(w), w)

        def _ste_bwd(w, g):
            mask = ((w > -1) & (w < 1)).astype(g.dtype)
            return (g * mask,)
        ste_sign.defvjp(_ste_fwd, _ste_bwd)
        key = jax.random.key(seed)
        k = jax.random.split(key, 6)
        B, S, H, O, E = (4, 512, 1024, 1024, 8)
        return {'x': jax.random.normal(k[0], (B, S, H), dtype=jnp.float32), 'weight': jax.random.normal(k[1], (O, H), dtype=jnp.float32) * 0.02, 'bias': jax.random.normal(k[2], (O,), dtype=jnp.float32) * 0.02, 'gate_w': jax.random.normal(k[3], (E, H), dtype=jnp.float32) * 0.02, 'in_channel_scale': jax.random.normal(k[4], (E, H), dtype=jnp.float32), 'out_channel_scale': jax.random.normal(k[5], (E, O), dtype=jnp.float32)}
    _L0_ffn_all = _L0_ffn_setup()
    _L0_ffn_in = {k: v for k, v in _L0_ffn_all.items() if k in ('weight', 'bias', 'gate_w', 'in_channel_scale', 'out_channel_scale')}
    del _L0_ffn_all

    def _L1_xattn_setup():
        import jax, jax.numpy as jnp
        import numpy as np
        TEXT_DIM = 1024
        FEATURE_DIM = 1024

        def _xavier_uniform(key, shape):
            fan_in, fan_out = (shape[1], shape[0])
            limit = float(np.sqrt(6.0 / (fan_in + fan_out)))
            return jax.random.uniform(key, shape, jnp.float32, -limit, limit)
        key = jax.random.key(seed)
        k1, k2, k3, k4 = jax.random.split(key, 4)
        text = jax.random.normal(k1, (8, 512, TEXT_DIM), jnp.float32)
        features = jax.random.normal(k2, (8, 144, FEATURE_DIM), jnp.float32)
        Wq = _xavier_uniform(k3, (FEATURE_DIM, TEXT_DIM))
        bq = jnp.zeros((FEATURE_DIM,), jnp.float32)
        Wk = _xavier_uniform(k4, (FEATURE_DIM, FEATURE_DIM))
        bk = jnp.zeros((FEATURE_DIM,), jnp.float32)
        return {'text': text, 'features': features, 'Wq': Wq, 'bq': bq, 'Wk': Wk, 'bk': bk}
    _L1_xattn_all = _L1_xattn_setup()
    _L1_xattn_in = {k: v for k, v in _L1_xattn_all.items() if k in ('Wq', 'bq', 'Wk', 'bk')}
    del _L1_xattn_all

    def _L1_ffn_setup():
        import jax, jax.numpy as jnp
        import numpy as np
        ALPHA = 32
        R = 16
        SCALING = ALPHA / R
        key = jax.random.key(seed)
        k1, k2, k3, k4 = jax.random.split(key, 4)
        B_, S, D = (4, 512, 1024)
        H, r, O = (8, R, 1024)
        x = jax.random.normal(k1, (B_, S, D), dtype=jnp.float32)
        A = jax.random.normal(k2, (H, r, D), dtype=jnp.float32) * 0.02
        Bm = jax.random.normal(k3, (H, O, r), dtype=jnp.float32) * 0.02
        Wr = jax.random.normal(k4, (H, D), dtype=jnp.float32) * 0.02
        br = jnp.zeros((H,), dtype=jnp.float32)
        return {'x': x, 'A': A, 'B': Bm, 'Wr': Wr, 'br': br}
    _L1_ffn_all = _L1_ffn_setup()
    _L1_ffn_in = {k: v for k, v in _L1_ffn_all.items() if k in ('A', 'B', 'Wr', 'br')}
    del _L1_ffn_all
    return {'x': x, 'ctx_4096': ctx_4096, 'L0_xattn_Wq': _L0_xattn_in['Wq'], 'L0_xattn_bq': _L0_xattn_in['bq'], 'L0_xattn_Wk': _L0_xattn_in['Wk'], 'L0_xattn_bk': _L0_xattn_in['bk'], 'L0_xattn_Wv': _L0_xattn_in['Wv'], 'L0_xattn_bv': _L0_xattn_in['bv'], 'L0_ffn_weight': _L0_ffn_in['weight'], 'L0_ffn_bias': _L0_ffn_in['bias'], 'L0_ffn_gate_w': _L0_ffn_in['gate_w'], 'L0_ffn_in_channel_scale': _L0_ffn_in['in_channel_scale'], 'L0_ffn_out_channel_scale': _L0_ffn_in['out_channel_scale'], 'L1_xattn_Wq': _L1_xattn_in['Wq'], 'L1_xattn_bq': _L1_xattn_in['bq'], 'L1_xattn_Wk': _L1_xattn_in['Wk'], 'L1_xattn_bk': _L1_xattn_in['bk'], 'L1_ffn_A': _L1_ffn_in['A'], 'L1_ffn_B': _L1_ffn_in['B'], 'L1_ffn_Wr': _L1_ffn_in['Wr'], 'L1_ffn_br': _L1_ffn_in['br']}

def reference(x, ctx_4096, L0_xattn_Wq, L0_xattn_bq, L0_xattn_Wk, L0_xattn_bk, L0_xattn_Wv, L0_xattn_bv, L0_ffn_weight, L0_ffn_bias, L0_ffn_gate_w, L0_ffn_in_channel_scale, L0_ffn_out_channel_scale, L1_xattn_Wq, L1_xattn_bq, L1_xattn_Wk, L1_xattn_bk, L1_ffn_A, L1_ffn_B, L1_ffn_Wr, L1_ffn_br):
    import jax
    import jax.numpy as jnp

    def _L0_xattn_ref(x, init, Wq, bq, Wk, bk, Wv, bv):
        import jax, jax.numpy as jnp
        import numpy as np
        B, C, T = (4, 128, 1024)
        DQK = 64
        q = jnp.einsum('dc,bct->btd', Wq, init) + bq
        k = jnp.einsum('dc,bct->bdt', Wk, init) + bk[None, :, None]
        R = jnp.einsum('btd,bds->bts', q, k)
        attention = jax.nn.softmax(R, axis=-1)
        v = jnp.einsum('oc,bct->bto', Wv, x) + bv
        out = jnp.einsum('bts,bsc->bct', attention, v)
        return out

    def _L0_ffn_ref(x, weight, bias, gate_w, in_channel_scale, out_channel_scale):
        import jax, jax.numpy as jnp
        import numpy as np

        @jax.custom_vjp
        def ste_sign(w):
            return jnp.sign(w)

        def _ste_fwd(w):
            return (jnp.sign(w), w)

        def _ste_bwd(w, g):
            mask = ((w > -1) & (w < 1)).astype(g.dtype)
            return (g * mask,)
        ste_sign.defvjp(_ste_fwd, _ste_bwd)
        B, S, H = x.shape
        xf = x.reshape(-1, H)
        router_logits = xf @ gate_w.T
        routing = jax.nn.softmax(router_logits.astype(jnp.float32), axis=1).astype(x.dtype)
        in_scale = routing @ in_channel_scale
        out_scale = routing @ out_channel_scale
        wb = ste_sign(weight)
        out = xf * in_scale @ wb.T * out_scale + bias
        return out.reshape(B, S, -1)

    def _L1_xattn_ref(text, features, Wq, bq, Wk, bk):
        import jax, jax.numpy as jnp
        import numpy as np
        TEXT_DIM = 1024
        FEATURE_DIM = 1024

        def _xavier_uniform(key, shape):
            fan_in, fan_out = (shape[1], shape[0])
            limit = float(np.sqrt(6.0 / (fan_in + fan_out)))
            return jax.random.uniform(key, shape, jnp.float32, -limit, limit)
        Q = jnp.einsum('btx,dx->btd', text, Wq) + bq
        K = jnp.einsum('bpx,dx->bpd', features, Wk) + bk
        scale = 1.0 / jnp.sqrt(jnp.asarray(K.shape[-1], K.dtype))
        scores = jnp.einsum('btd,bpd->btp', Q, K) * scale
        attn = jax.nn.softmax(scores, axis=-1)
        attended = jnp.einsum('btp,bpd->btd', attn, features)
        return attended

    def _L1_ffn_ref(x, A, B, Wr, br):
        import jax, jax.numpy as jnp
        import numpy as np
        ALPHA = 32
        R = 16
        SCALING = ALPHA / R
        H = A.shape[0]
        router_logits = jnp.einsum('bsd,hd->bsh', x, Wr) + br
        scores = H * jax.nn.softmax(router_logits, axis=-1)
        low = jnp.einsum('bsd,hrd->bshr', x, A)
        out = jnp.einsum('bshr,hor,bsh->bso', low, B, scores)
        return SCALING * out
    x = x + _L0_xattn_ref(_layernorm(x, axis=-1), ctx_4096, L0_xattn_Wq, L0_xattn_bq, L0_xattn_Wk, L0_xattn_bk, L0_xattn_Wv, L0_xattn_bv)
    x = x + _L0_ffn_ref(_layernorm(x, axis=-1), L0_ffn_weight, L0_ffn_bias, L0_ffn_gate_w, L0_ffn_in_channel_scale, L0_ffn_out_channel_scale)
    x = x + _L1_xattn_ref(_layernorm(x, axis=-1), ctx_4096, L1_xattn_Wq, L1_xattn_bq, L1_xattn_Wk, L1_xattn_bk)
    x = x + _L1_ffn_ref(_layernorm(x, axis=-1), L1_ffn_A, L1_ffn_B, L1_ffn_Wr, L1_ffn_br)
    return x

_drawn_inputs = setup_inputs


def setup_inputs(seed=0):
    import zlib

    import numpy as np

    out = dict(_drawn_inputs(seed))
    spreads = {'L1_xattn_bq': (0.0, 2.0), 'L1_xattn_bk': (0.0, 2.0), 'L1_ffn_br': (0.0, 2.0)}
    factors = {'L0_xattn_bk': 64.0, 'L0_xattn_bv': 3.514, 'L0_ffn_bias': 8.0}
    for name, (base, spread) in spreads.items():
        noise = np.random.default_rng([zlib.crc32(name.encode()), seed]).standard_normal(out[name].shape)
        drawn = base * np.exp(spread * noise) if base else spread * noise
        out[name] = jnp.asarray(drawn.astype(out[name].dtype))
    for name, factor in factors.items():
        out[name] = (out[name] * factor).astype(out[name].dtype)
    return out
```

```python
from contextlib import ExitStack

import concourse.bass as bass
from concourse import mybir

F32 = mybir.dt.float32
F32R = mybir.dt.float32r
ALU = mybir.AluOpType
ACT = mybir.ActivationFunctionType
AX_X = mybir.AxisListType.X

P = 128
HALF = 512
EPS = 1e-5


class Steps:

    def __init__(self, sem, per):
        self.sem, self.per = sem, per

    def begin(self, b):
        self.base, self.n = b * self.per, 0

    def chain(self, engine, instruction):
        self.n += 1
        instruction.then_inc(self.sem, 1)
        engine.wait_ge(self.sem, self.base + self.n)

    def end(self):
        assert self.n == self.per, (self.n, self.per)


def build(nc, x, ctx_, wq0, bq0, wk0, bk0, wv0, bv0, w_ffn, b_ffn, gate, ics, ocs,
          wq1, bq1, wk1, bk1, a1, b1, wr1, br1, out):
    NB, S, D = x.shape
    DQK = wq0.shape[0]
    E = gate.shape[0]
    R = a1.shape[1]
    HR = E * R
    T = D // P
    SCALE1 = float(D) ** -0.5
    LORA = 2.0 * E
    assert S == P and HR == P and 2 * DQK == P and D == 2 * HALF

    top = ExitStack()
    with top:
        def sb(name, shape, dt=F32, stack=top):
            return stack.enter_context(nc.sbuf_tensor(name, shape, dt))

        def sem(name, stack=top):
            return stack.enter_context(nc.semaphore(name))

        ident = sb("ident", [P, P])
        ones = sb("ones", [P, T])
        minus_half = sb("minus_half", [P, 1])
        wqT = sb("wqT", [P, P])
        wkT = sb("wkT", [P, P])
        wvT = sb("wvT", [P, P])
        bq_col = sb("bq_col", [P, 1])
        bk_col = sb("bk_col", [P, 1])
        bv_col = sb("bv_col", [P, 1])
        signT = sb("signT", [P, T, D], F32R)
        gateT = sb("gateT", [P, T, 2 * E])
        ics3 = sb("ics3", [96, D], F32R)
        ocs3 = sb("ocs3", [96, D], F32R)
        bias_rows = sb("bias_rows", [P, D])
        mT = sb("mT", [P, T, D])
        key_bias = sb("key_bias", [P, T])
        query_bias = sb("query_bias", [P, D])
        bqbk = sb("bqbk", [P, 1])
        lowT = sb("lowT", [P, T, HR + E])
        bT = sb("bT", [P, D])
        br_rows = sb("br_rows", [P, E])

        with ExitStack() as tmp:
            wq_nat = sb("wq_nat", [P, T, D], F32, tmp)
            wk_nat = sb("wk_nat", [P, T, D], F32, tmp)
            wf_nat = sb("wf_nat", [P, T, D], F32, tmp)
            small = sb("small", [P, 3, P], F32, tmp)
            a_nat = sb("a_nat", [P, D], F32, tmp)
            g_nat = sb("g_nat", [2 * E, D], F32, tmp)
            b_nat = sb("b_nat", [P, T, E, R], F32, tmp)
            bq1_col = sb("bq1_col", [P, T], F32, tmp)
            bk1_col = sb("bk1_col", [P, T], F32, tmp)
            ics_f = query_bias[0:96, :]
            ocs_f = sb("ocs_f", [96, D], F32, tmp)
            bank = [tmp.enter_context(nc.psum_tensor(f"setup{i}", [P, HALF], F32)) for i in range(8)]
            zeroed = sem("zeroed", tmp)
            ident_made = sem("ident_made", tmp)
            small_in = sem("small_in", tmp)
            ffn_in = sem("ffn_in", tmp)
            scales_in = sem("scales_in", tmp)
            low_in = sem("low_in", tmp)
            qk_in = sem("qk_in", tmp)
            filled = sem("filled", tmp)
            signed = sem("signed", tmp)
            copied = sem("copied", tmp)
            split = sem("split", tmp)

            groups = ([("small", 0), ("gate", 0)] + [("low", 0), ("low", 1), ("b", 0), ("b", 1)]
                      + [("sign", i) for i in range(2 * T)] + [("m", i) for i in range(2 * T)]
                      + [("rows", 0), ("rows", 1), ("bias", 0)])

            with nc.Block() as block:
                @block.sync
                def _(sp):
                    n_small = 0
                    for dst, src in (
                        (small[0:DQK, 0, :], wq0), (small[DQK:P, 0, :], wq0),
                        (small[0:DQK, 1, :], wk0), (small[DQK:P, 1, :], wk0), (small[:, 2, :], wv0),
                        (bq_col[0:DQK, :], bq0.unsqueeze(1)), (bq_col[DQK:P, :], bq0.unsqueeze(1)),
                        (bk_col[0:DQK, :], bk0.unsqueeze(1)), (bk_col[DQK:P, :], bk0.unsqueeze(1)),
                        (bv_col[:, :], bv0.unsqueeze(1)),
                        (g_nat[0:E, :], gate), (g_nat[E:2 * E, :], wr1),
                        (bias_rows[:, :], b_ffn.partition_broadcast(P)),
                        (br_rows[:, :], br1.partition_broadcast(P)),
                    ):
                        sp.dma_start(dst, src).then_inc(small_in, 16)
                        n_small += 1
                    assert n_small == 14
                    sp.dma_start(a_nat[:, :], a1.rearrange("h r d -> (h r) d")).then_inc(low_in, 16)
                    for h in range(E):
                        sp.dma_start(b_nat[:, :, h, :], b1[h].rearrange("(t p) r -> p t r", p=P)).then_inc(low_in, 16)
                    sp.wait_ge(zeroed, 2)
                    for k in range(3):
                        sp.dma_start(ics_f[32 * k:32 * k + E, :], ics).then_inc(scales_in, 16)
                        sp.dma_start(ocs_f[32 * k:32 * k + E, :], ocs).then_inc(scales_in, 16)
                    sp.dma_start(wf_nat[:, :, :], w_ffn.rearrange("(t p) h -> p t h", p=P)).then_inc(ffn_in, 16)

                @block.gpsimd
                def _(pool):
                    nc.gpsimd.memset(ident[:, :], 0.0).then_inc(ident_made, 1)
                    pool.wait_ge(ident_made, 1)
                    nc.gpsimd.affine_select(out=ident[:, :], in_=ident[:, :], compare_op=ALU.not_equal, fill=1.0,
                                            base=0, pattern=[[-1, P]], channel_multiplier=1).then_inc(ident_made, 1)
                    nc.gpsimd.memset(ones[:, :], 1.0)
                    nc.gpsimd.memset(minus_half[:, :], -0.5)

                @block.scalar
                def _(act):
                    act.dma_start(wk_nat[:, :, :], wk1.rearrange("(t p) x -> p t x", p=P)).then_inc(qk_in, 16)
                    act.dma_start(wq_nat[:, :, :], wq1.rearrange("(t p) x -> p t x", p=P)).then_inc(qk_in, 16)
                    act.dma_start(bq1_col[:, :], bq1.rearrange("(t p) -> p t", p=P), allow_slow_non_contiguous=True).then_inc(qk_in, 16)
                    act.dma_start(bk1_col[:, :], bk1.rearrange("(t p) -> p t", p=P), allow_slow_non_contiguous=True).then_inc(qk_in, 16)
                    for n, (kind, i) in enumerate(groups):
                        if kind != "sign":
                            continue
                        act.wait_ge(filled, n + 1)
                        nc.scalar.activation(signT[:, i // 2, (i % 2) * HALF:(i % 2 + 1) * HALF], bank[n % 8][:, :],
                                             ACT.Sign).then_inc(signed, 1)

                @block.vector
                def _(dve):
                    nc.vector.memset(ics_f, 0.0).then_inc(zeroed, 1)
                    nc.vector.memset(ocs_f[:, :], 0.0).then_inc(zeroed, 1)
                    dve.wait_ge(scales_in, 6 * 16)
                    nc.vector.tensor_copy(ics3[:, :], ics_f).then_inc(split, 1)
                    nc.vector.tensor_copy(ocs3[:, :], ocs_f[:, :]).then_inc(split, 1)
                    dve.wait_ge(split, 2)
                    for hi, full in ((ics3, query_bias), (ocs3, ocs_f)):
                        nc.vector.tensor_tensor(hi[64:96, :], full[64:96, :], hi[64:96, :].bitcast(F32), ALU.subtract).then_inc(split, 1)
                    for n, (kind, i) in enumerate(groups):
                        if kind == "sign":
                            continue
                        dve.wait_ge(filled, n + 1)
                        s = bank[n % 8]
                        if kind == "small":
                            nc.vector.tensor_copy(wqT[:, :], s[:, 0:P])
                            nc.vector.tensor_copy(wkT[:, :], s[:, P:2 * P])
                            last = nc.vector.tensor_copy(wvT[:, :], s[:, 2 * P:3 * P])
                        elif kind == "gate":
                            nc.vector.tensor_copy(gateT[:, :, :], s[:, 0:T * 2 * E].rearrange("p (t e) -> p t e", t=T))
                            last = nc.vector.tensor_copy(
                                lowT[:, :, HR:HR + E], s[:, 0:T * 2 * E].rearrange("p (t e) -> p t e", t=T)[:, :, E:2 * E])
                        elif kind == "low":
                            last = nc.vector.tensor_copy(lowT[:, 4 * i:4 * i + 4, 0:HR],
                                                         s[:, :].rearrange("p (t e) -> p t e", t=4))
                        elif kind == "b":
                            last = nc.vector.tensor_copy(bT[:, i * HALF:(i + 1) * HALF], s[:, :])
                        elif kind == "m":
                            last = nc.vector.tensor_copy(mT[:, i // 2, (i % 2) * HALF:(i % 2 + 1) * HALF], s[:, :])
                        elif kind == "rows":
                            if i == 0:
                                dve.wait_ge(split, 4)
                            last = nc.vector.tensor_copy(query_bias[:, i * HALF:(i + 1) * HALF], s[:, :])
                        else:
                            nc.vector.tensor_copy(key_bias[:, :], s[:, 0:T])
                            last = nc.vector.tensor_copy(bqbk[:, :], s[:, T:T + 1])
                        last.then_inc(copied, 1)

                @block.tensor
                def _(pe):
                    pe.wait_ge(ident_made, 2)
                    pe.wait_ge(small_in, 14 * 16)
                    for n, (kind, i) in enumerate(groups):
                        if n >= 8:
                            by_act = groups[n - 8][0] == "sign"
                            pe.wait_ge(signed if by_act else copied,
                                       sum((g[0] == "sign") == by_act for g in groups[:n - 7]))
                        s = bank[n % 8]
                        if kind == "small":
                            for j in range(3):
                                last = nc.tensor.transpose(s[:, j * P:(j + 1) * P], small[:, j, :], ident[:, :])
                        elif kind == "gate":
                            for t in range(T):
                                last = nc.tensor.transpose(s[:, t * 2 * E:(t + 1) * 2 * E], g_nat[:, t * P:(t + 1) * P],
                                                           ident[0:2 * E, 0:2 * E])
                        elif kind == "low":
                            if i == 0:
                                pe.wait_ge(low_in, 16 * (1 + E))
                            for j in range(4):
                                t = 4 * i + j
                                last = nc.tensor.transpose(s[:, j * P:(j + 1) * P], a_nat[:, t * P:(t + 1) * P], ident[:, :])
                        elif kind == "b":
                            for j in range(4):
                                last = nc.tensor.transpose(s[:, j * P:(j + 1) * P],
                                                           b_nat[:, 4 * i + j, :, :].rearrange("p h r -> p (h r)"), ident[:, :])
                        elif kind == "sign":
                            if i == 0:
                                pe.wait_ge(ffn_in, 16)
                            for j in range(4):
                                to = 4 * (i % 2) + j
                                last = nc.tensor.transpose(s[:, j * P:(j + 1) * P],
                                                           wf_nat[:, to, (i // 2) * P:(i // 2 + 1) * P], ident[:, :])
                        elif kind == "m":
                            if i == 0:
                                pe.wait_ge(qk_in, 4 * 16)
                            for t in range(T):
                                last = nc.tensor.matmul(s[:, :], wk_nat[:, t, (i // 2) * P:(i // 2 + 1) * P],
                                                        wq_nat[:, t, (i % 2) * HALF:(i % 2 + 1) * HALF],
                                                        start=t == 0, stop=t == T - 1)
                        elif kind == "rows":
                            for t in range(T):
                                last = nc.tensor.matmul(s[:, :], bq1_col[:, t:t + 1].to_broadcast([P, P]),
                                                        wk_nat[:, t, i * HALF:(i + 1) * HALF], start=t == 0, stop=t == T - 1)
                        else:
                            for j in range(T):
                                for t in range(T):
                                    nc.tensor.matmul(s[:, j:j + 1], wq_nat[:, t, j * P:(j + 1) * P], bk1_col[:, t:t + 1],
                                                     start=t == 0, stop=t == T - 1)
                            for t in range(T):
                                last = nc.tensor.matmul(s[:, T:T + 1], bq1_col[:, t:t + 1].to_broadcast([P, P]),
                                                        bk1_col[:, t:t + 1], start=t == 0, stop=t == T - 1)
                        last.then_inc(filled, 1)

        c_in = sb("c_in", [P, D])
        xn = sb("xn", [P, D])
        v_hi = sb("v_hi", [P, T, P], F32R)
        v_lo = sb("v_lo", [P, T, P], F32R)
        q_hl = sb("q_hl", [P, D], F32R)
        q_hm = sb("q_hm", [DQK + 1, D], F32R)
        k_hh = sb("k_hh", [P, D], F32R)
        k_l1 = sb("k_l1", [DQK + 1, D], F32R)
        cT = sb("cT", [P, T, P])
        neg_max = sb("neg_max", [P, DQK + T])
        prob = [sb(f"prob{i}", [P, D]) for i in range(2)]
        p_hi = [sb(f"p_hi{i}", [P, D], F32R) for i in range(2)]
        p_lo = [sb(f"p_lo{i}", [P, D], F32R) for i in range(2)]
        p_sum = sb("p_sum", [P, D])
        x1 = sb("x1", [P, D])
        kw = sb("kw", [P, D])
        kwT = sb("kwT", [P, T, P])
        den_inv = sb("den_inv", [P, T])
        den_rows = sb("den_rows", [P, D])
        res = sb("res", [P, D])
        xn_c = sb("xn_c", [P, D])
        xnT = sb("xnT", [P, T, P])
        y_hi = sb("y_hi", [P, T, P], F32R)
        y_lo = sb("y_lo", [P, T, P], F32R)
        oscale = sb("oscale", [P, D])
        c_val = sb("c_val", [P, D])
        stat = [sb(f"stat{i}", [P, 12]) for i in range(4)]
        mean_var = [sb(f"mean_var{i}", [P, 2]) for i in range(4)]
        neg_mean = [sb(f"neg_mean{i}", [P, 1]) for i in range(4)]
        var_eps = [sb(f"var_eps{i}", [P, 1]) for i in range(4)]
        rstd = [sb(f"rstd{i}", [P, 1]) for i in range(4)]
        shift = [sb(f"shift{i}", [P, 1]) for i in range(4)]
        logit = sb("logit", [P, E])
        r_max = [sb(f"r_max{i}", [P, 1]) for i in range(3)]
        r_bias = sb("r_bias", [P, 1])
        r_exp = [sb(f"r_exp{i}", [P, E]) for i in range(2)]
        r_sum = [sb(f"r_sum{i}", [P, 1]) for i in range(3)]
        r_inv = [sb(f"r_inv{i}", [P, 1]) for i in range(3)]
        route = sb("route", [P, E])
        route1 = sb("route1", [P, E])
        route3 = sb("route3", [P, 96], F32R)
        route3T = sb("route3T", [96, P], F32R)
        key_sum = sb("key_sum", [P, 1])
        key_col = sb("key_col", [P, 1])
        result = sb("result", [P, D])
        attn = sb("attn", [P, P])
        attnT = sb("attnT", [P, P])
        low = sb("low", [P, HR])
        low_T = sb("low_T", [P, P])

        def psum(name, shape):
            return top.enter_context(nc.psum_tensor(name, shape, F32))

        scores = [psum(f"scores{i}", [P, D]) for i in range(2)]
        acc = psum("acc", [P, D])
        shared = [psum(f"shared{i}", [P, HALF]) for i in range(2)]

        const_made = sem("const_made")
        c_loaded = sem("c_loaded")
        xn_loaded = sem("xn_loaded")
        x1_loaded = sem("x1_loaded")
        val_loaded = sem("val_loaded")
        stored = sem("stored")
        var_ready = [sem(f"var_ready{i}") for i in range(4)]
        shift_ready = [sem(f"shift_ready{i}") for i in range(4)]
        normed = [sem(f"normed{i}") for i in range(4)]
        cT_done = sem("cT_done")
        q_done = sem("q_done")
        k_done = sem("k_done")
        v_done = sem("v_done")
        maxscores_done = sem("maxscores_done")
        kw_done = sem("kw_done")
        max_turned = sem("max_turned")
        scores_done = sem("scores_done")
        pv_done = sem("pv_done")
        den_done = sem("den_done")
        den_turned = sem("den_turned")
        kwT_done = sem("kwT_done")
        xnT_done = [None] + [sem(f"xnT_done{i}") for i in (1, 2, 3)]
        route_done = sem("route_done")
        routeT_done = sem("routeT_done")
        iscale_done = sem("iscale_done")
        oscale_done = sem("oscale_done")
        ffn_done = sem("ffn_done")
        sc1_done = sem("sc1_done")
        attnT_done = sem("attnT_done")
        att_done = sem("att_done")
        low_done = sem("low_done")
        lowT_done = sem("lowT_done")
        out_done = sem("out_done")
        cT_a_ready = sem("cT_a_ready")
        cT_b_ready = sem("cT_b_ready")
        k_hi_ready = sem("k_hi_ready")
        q_hi_ready = sem("q_hi_ready")
        q_ready = sem("q_ready")
        k_ready = sem("k_ready")
        v_hi_ready = sem("v_hi_ready")
        v_ready = sem("v_ready")
        row_max = sem("row_max")
        kw_ready = sem("kw_ready")
        max_ready = sem("max_ready")
        exp_ready = sem("exp_ready")
        p_hi_ready = sem("p_hi_ready")
        p_lo_ready = sem("p_lo_ready")
        p_summed = sem("p_summed")
        den_inv_ready = sem("den_inv_ready")
        den_rows_ready = sem("den_rows_ready")
        x1_ready = sem("x1_ready")
        kwT_ready = sem("kwT_ready")
        key_col_ready = sem("key_col_ready")
        xnT_a_ready = [None] + [sem(f"xnT_a_ready{i}") for i in (1, 2, 3)]
        xnT_b_ready = [None] + [sem(f"xnT_b_ready{i}") for i in (1, 2, 3)]
        biased = sem("biased")
        r_max_ready = sem("r_max_ready")
        r_exp_ready = sem("r_exp_ready")
        route_ready = sem("route_ready")
        routeT_ready = sem("routeT_ready")
        y_ready = sem("y_ready")
        y_hi_ready = sem("y_hi_ready")
        y_lo_ready = sem("y_lo_ready")
        oscale_ready = sem("oscale_ready")
        x2_ready = sem("x2_ready")
        s_max_ready = sem("s_max_ready")
        attn_ready = sem("attn_ready")
        attnT_ready = sem("attnT_ready")
        x3_ready = sem("x3_ready")
        l_max_ready = sem("l_max_ready")
        l_exp_ready = sem("l_exp_ready")
        low_ready = sem("low_ready")
        lowT_ready = sem("lowT_ready")
        out_ready = sem("out_ready")
        dve_prepare = Steps(sem("dve_prepare"), 2)
        dve_attend = Steps(sem("dve_attend"), 4)
        dve_chain = Steps(sem("dve_chain"), 14)
        pool_norm = [Steps(sem(f"pool_norm{i}"), 1) for i in range(4)]
        act_chain = Steps(sem("act_chain"), 1)

        def half(h):
            return slice(h * HALF, (h + 1) * HALF)

        def tile4(buf, h):
            return buf[:, 4 * h:4 * h + 4, :].rearrange("p t c -> p (t c)")

        def nth(per, b, n):
            if isinstance(b, int):
                return max(0, per * min(b, NB - 1) + n)
            return b * per + n

        def iterations(engine, body):
            for k in range(3):
                body(k, True, k >= 1, k >= 2)
            with engine.Fori(3, NB) as k:
                body(k, True, True, True)
            body(NB, False, True, True)
            body(NB + 1, False, False, True)

        with nc.Block() as block:

            @block.sync
            def _(sp):
                def body(k, prepare, attend, chain):
                    b, a, c = k, k - 1, k - 2
                    if prepare:
                        sp.wait_ge(k_done, nth(2, b - 1, 2))
                        sp.dma_start(c_in[:, :], ctx_[b]).then_inc(c_loaded, 16)
                        sp.wait_ge(v_done, nth(2, b - 1, 2))
                        sp.dma_start(xn[:, :], x[b]).then_inc(xn_loaded, 16)
                    if attend:
                        sp.wait_ge(normed[1], nth(1, a - 1, 1))
                        sp.wait_ge(biased, nth(1, a - 1, 1))
                        sp.dma_start(x1[:, :], x[a]).then_inc(x1_loaded, 16)
                    if chain:
                        sp.wait_ge(att_done, nth(2, c - 1, 2))
                        sp.dma_start(c_val[:, :], ctx_[c]).then_inc(val_loaded, 16)
                        sp.wait_ge(out_ready, nth(2, c, 2))
                        sp.dma_start(out[c], result[:, :]).then_inc(stored, 16)

                iterations(sp, body)
                sp.wait_ge(stored, 16 * NB)

            @block.gpsimd
            def _(pool):
                def norm_scale(i, b):
                    pool.wait_ge(var_ready[i], nth(1, b, 1))
                    pool.wait_ge(normed[i], nth(1, b - 1, 1))
                    pool_norm[i].begin(b)
                    pool_norm[i].chain(pool, nc.gpsimd.tensor_tensor(rstd[i][:, :], var_eps[i][:, :], minus_half[:, :], ALU.pow))
                    nc.gpsimd.tensor_tensor(shift[i][:, :], neg_mean[i][:, :], rstd[i][:, :], ALU.mult).then_inc(shift_ready[i], 1)
                    pool_norm[i].end()

                def body(k, prepare, attend, chain):
                    b, a, c = k, k - 1, k - 2
                    if chain:
                        pool.wait_ge(x1_ready, nth(2, c, 2))
                        pool.wait_ge(out_ready, nth(2, c - 1, 2))
                        nc.gpsimd.tensor_tensor(res[:, :], x1[:, :], bias_rows[:, :], ALU.add).then_inc(biased, 1)
                    if prepare:
                        norm_scale(0, b)
                    for s in range(T):
                        if attend and s >= 1:
                            pool.wait_ge(exp_ready, nth(8, a, s + 1))
                            if s == 1:
                                pool.wait_ge(den_done, nth(1, a - 1, 1))
                                nc.gpsimd.tensor_tensor(p_sum[:, :], prob[0][:, :], prob[1][:, :], ALU.add).then_inc(p_summed, 1)
                            else:
                                pool.wait_ge(p_summed, nth(7, a, s - 1))
                                nc.gpsimd.tensor_tensor(p_sum[:, :], p_sum[:, :], prob[s % 2][:, :], ALU.add).then_inc(p_summed, 1)
                        if chain and s == 2:
                            norm_scale(2, c)
                    if chain:
                        norm_scale(3, c)
                    if attend:
                        norm_scale(1, a)

                iterations(pool, body)

            @block.scalar
            def _(act):
                def normalize(i, b, to, src):
                    act.wait_ge(shift_ready[i], nth(1, b, 1))
                    nc.scalar.activation(to[:, :], src[:, :], ACT.Identity, bias=shift[i][:, :],
                                         scale=rstd[i][:, :]).then_inc(normed[i], 1)

                def transposed_half(i, c):
                    act.wait_ge(xnT_done[i], nth(2, c, 1))
                    nc.scalar.activation(tile4(xnT, 0), shared[0][:, :], ACT.Identity).then_inc(xnT_a_ready[i], 1)

                def body(k, prepare, attend, chain):
                    b, a, c = k, k - 1, k - 2
                    if chain:
                        act.wait_ge(xnT_done[3], nth(2, c - 1, 2))
                        normalize(1, c, xn_c, x1)
                        act.wait_ge(low_done, nth(1, c - 1, 1))
                        transposed_half(1, c)
                    if attend:
                        act.wait_ge(kw_done, nth(2, a, 1))
                        act.wait_ge(kwT_done, nth(2, a - 1, 2))
                        nc.scalar.activation(kw[:, half(0)], acc[:, half(0)], ACT.Identity).then_inc(kw_ready, 1)
                    if prepare:
                        normalize(0, b, xn, xn)
                    if chain:
                        act.wait_ge(r_max_ready, nth(1, c, 1))
                        nc.scalar.activation(r_exp[0][:, :], shared[0][:, 0:E], ACT.Exp, bias=r_max[0][:, :],
                                             accum_out=r_sum[0][:, :]).then_inc(r_exp_ready, 1)
                        act.wait_ge(routeT_done, nth(1, c, 1))
                        act.wait_ge(oscale_done, nth(2, c - 1, 2))
                        nc.scalar.activation(route3T[:, :], shared[1][0:96, 0:P], ACT.Identity).then_inc(routeT_ready, 1)
                        for h in range(2):
                            act.wait_ge(y_ready, nth(2, c, h + 1))
                            act.wait_ge(ffn_done, nth(2, c - 1, 2))
                            nc.scalar.activation(tile4(y_hi, h), tile4(xnT, h), ACT.Identity).then_inc(y_hi_ready, 1)
                    if attend:
                        act.wait_ge(kw_done, nth(2, a, 2))
                        nc.scalar.activation(kw[:, half(1)], acc[:, half(1)], ACT.Identity).then_inc(kw_ready, 1)
                    if chain:
                        for h in range(2):
                            act.wait_ge(oscale_done, nth(2, c, h + 1))
                            act.wait_ge(x2_ready, nth(2, c - 1, 2))
                            nc.scalar.activation(oscale[:, half(h)], shared[h][:, :], ACT.Identity).then_inc(oscale_ready, 1)
                    if attend:
                        for h in range(2):
                            act.wait_ge(max_turned, nth(2, a, h + 1))
                            nc.scalar.activation(q_hm[DQK:DQK + 1, half(h)], scores[0][DQK:DQK + 1, half(h)],
                                                 ACT.Identity).then_inc(max_ready, 1)
                    for s in range(T):
                        if attend:
                            act.wait_ge(scores_done, nth(8, a, s + 1))
                            act.wait_ge(p_lo_ready, nth(8, a, s - 1))
                            act.wait_ge(p_summed, nth(7, a, (-1, 0, 1)[s] if s < 3 else s - 2))
                            nc.scalar.activation(prob[s % 2][:, :], scores[s % 2][:, :], ACT.Exp).then_inc(exp_ready, 1)
                        if chain and s == 3:
                            act.wait_ge(xnT_done[1], nth(2, c, 2))
                            normalize(2, c, xn_c, res)
                        if chain and s == 5:
                            act.wait_ge(y_lo_ready, nth(2, c, 2))
                            transposed_half(2, c)
                        if chain and s == 6:
                            act_chain.begin(c)
                            act.wait_ge(s_max_ready, nth(1, c, 1))
                            act_chain.chain(act, nc.scalar.activation(r_bias[:, :], r_max[1][:, :], ACT.Identity, scale=SCALE1))
                            act_chain.end()
                            act.wait_ge(attnT_done, nth(1, c - 1, 1))
                            nc.scalar.activation(attn[:, :], shared[0][:, 0:P], ACT.Exp, bias=r_bias[:, :], scale=SCALE1,
                                                 accum_out=r_sum[1][:, :]).then_inc(attn_ready, 1)
                        if chain and s == 7:
                            act.wait_ge(attnT_done, nth(1, c, 1))
                            act.wait_ge(att_done, nth(2, c - 1, 2))
                            nc.scalar.activation(attnT[:, :], shared[1][:, 0:P], ACT.Identity).then_inc(attnT_ready, 1)
                    if prepare:
                        for h in range(2):
                            act.wait_ge(q_done, nth(2, b, h + 1))
                            nc.scalar.activation(q_hl[:, half(h)], scores[0][:, half(h)], ACT.Identity, bias=bq_col[:, :])
                            nc.scalar.activation(q_hm[0:DQK, half(h)], scores[0][0:DQK, half(h)], ACT.Identity,
                                                 bias=bq_col[0:DQK, :]).then_inc(q_hi_ready, 1)
                        act.wait_ge(cT_done, nth(2, b, 1))
                        act.wait_ge(kw_done, nth(2, b - 1, 2))
                        nc.scalar.activation(tile4(cT, 0), shared[0][:, :], ACT.Identity).then_inc(cT_a_ready, 1)
                    if chain:
                        act.wait_ge(xnT_done[2], nth(2, c, 2))
                        normalize(3, c, xn_c, res)
                    if prepare:
                        for h in range(2):
                            act.wait_ge(k_done, nth(2, b, h + 1))
                            nc.scalar.activation(k_hh[:, half(h)], scores[1][:, half(h)], ACT.Identity,
                                                 bias=bk_col[:, :]).then_inc(k_hi_ready, 1)
                    if chain:
                        act.wait_ge(sc1_done, nth(1, c, 1))
                        transposed_half(3, c)
                    if chain:
                        act.wait_ge(l_max_ready, nth(1, c, 1))
                        nc.scalar.activation(r_exp[1][:, :], logit[:, :], ACT.Exp, bias=r_max[2][:, :],
                                             accum_out=r_sum[2][:, :]).then_inc(l_exp_ready, 1)
                    if prepare:
                        for h in range(2):
                            act.wait_ge(v_done, nth(2, b, h + 1))
                            act.wait_ge(pv_done, nth(8, b - 1, 8))
                            nc.scalar.activation(tile4(v_hi, h), scores[0][:, half(h)], ACT.Identity).then_inc(v_hi_ready, 1)
                    if chain:
                        act.wait_ge(lowT_done, nth(1, c, 1))
                        act.wait_ge(out_done, nth(2, c - 1, 2))
                        nc.scalar.activation(low_T[:, :], shared[1][:, 0:P], ACT.Identity).then_inc(lowT_ready, 1)
                    if attend:
                        for h in range(2):
                            act.wait_ge(den_turned, nth(2, a, h + 1))
                            act.wait_ge(x1_ready, nth(2, a - 1, 2))
                            nc.scalar.activation(den_rows[:, half(h)], shared[h][:, :], ACT.Identity).then_inc(den_rows_ready, 1)

                iterations(act, body)

            @block.vector
            def _(dve):
                nc.vector.memset(k_l1[DQK:DQK + 1, :].bitcast(F32), 1.0).then_inc(const_made, 1)
                nc.vector.memset(neg_max[:, :], 0.0).then_inc(const_made, 1)
                nc.vector.memset(route3[:, :].bitcast(F32), 0.0).then_inc(const_made, 1)
                dve.wait_ge(const_made, 3)

                def statistics(steps, i, b, src):
                    dve.wait_ge(shift_ready[i], nth(1, b - 1, 1))
                    nc.vector.bn_stats(stat[i][:, 0:6], src[:, half(0)])
                    steps.chain(dve, nc.vector.bn_stats(stat[i][:, 6:12], src[:, half(1)]))
                    nc.vector.memset(var_eps[i][:, :], EPS)
                    steps.chain(dve, nc.vector.bn_aggr(mean_var[i][:, :], stat[i][:, :]))
                    nc.vector.tensor_scalar(neg_mean[i][:, :], mean_var[i][:, 0:1], -1.0, None, ALU.mult)
                    nc.vector.tensor_tensor(var_eps[i][:, :], mean_var[i][:, 1:2], var_eps[i][:, :], ALU.add).then_inc(var_ready[i], 1)

                def row_maximum(a, t):
                    dve.wait_ge(maxscores_done, nth(8, a, t + 1))
                    dve.wait_ge(max_turned, nth(2, a - 1, 2))
                    nc.vector.tensor_reduce(neg_max[:, DQK + t:DQK + t + 1], scores[t % 2][:, :], AX_X, ALU.max,
                                            negate=True).then_inc(row_max, 1)

                def transposed_half(i, c):
                    dve.wait_ge(xnT_done[i], nth(2, c, 2))
                    nc.vector.tensor_copy(tile4(xnT, 1), shared[1][:, :]).then_inc(xnT_b_ready[i], 1)

                def half_of_x2(c, h):
                    dve.wait_ge(ffn_done, nth(2, c, h + 1))
                    dve.wait_ge(oscale_ready, nth(2, c, h + 1))
                    dve_chain.chain(dve, nc.vector.tensor_tensor(oscale[:, half(h)], shared[h][:, :], oscale[:, half(h)], ALU.mult))
                    nc.vector.tensor_tensor(res[:, half(h)], res[:, half(h)], oscale[:, half(h)], ALU.add).then_inc(x2_ready, 1)

                def body(k, prepare, attend, chain):
                    b, a, c = k, k - 1, k - 2
                    if chain:
                        dve_chain.begin(c)
                    if attend:
                        dve_attend.begin(a)
                        row_maximum(a, 0)
                        row_maximum(a, 1)
                        row_maximum(a, 2)
                    if chain:
                        dve.wait_ge(low_done, nth(1, c - 1, 1))
                        transposed_half(1, c)
                    if prepare:
                        dve.wait_ge(xn_loaded, nth(16, b, 16))
                        dve_prepare.begin(b)
                        statistics(dve_prepare, 0, b, xn)
                        dve_prepare.end()
                    if attend:
                        row_maximum(a, 3)
                        row_maximum(a, 4)
                    if chain:
                        dve.wait_ge(route_done, nth(1, c, 1))
                        nc.vector.tensor_reduce(r_max[0][:, :], shared[0][:, 0:E], AX_X, ALU.max,
                                                negate=True).then_inc(r_max_ready, 1)
                    if attend:
                        row_maximum(a, 5)
                    if chain:
                        dve.wait_ge(r_exp_ready, nth(1, c, 1))
                        dve_chain.chain(dve, nc.vector.reciprocal(r_inv[0][:, :], r_sum[0][:, :]))
                        dve_chain.chain(dve, nc.vector.tensor_scalar(route[:, :], r_exp[0][:, :], r_inv[0][:, :], None, ALU.mult))
                        dve.wait_ge(routeT_done, nth(1, c - 1, 1))
                        nc.vector.tensor_copy(route3[:, 0:E], route[:, :])
                        dve_chain.chain(dve, nc.vector.tensor_copy(route3[:, 64:64 + E], route[:, :]))
                        nc.vector.tensor_tensor(route3[:, 32:32 + E], route[:, :], route3[:, 0:E].bitcast(F32),
                                                ALU.subtract).then_inc(route_ready, 1)
                        dve.wait_ge(val_loaded, nth(16, c, 16))
                        dve.wait_ge(sc1_done, nth(1, c - 1, 1))
                        dve_chain.chain(dve, nc.vector.tensor_tensor_reduce(
                            out=den_rows[:, :], in0=c_val[:, :], in1=query_bias[:, :], scale=1.0, scalar=0.0,
                            op0=ALU.mult, op1=ALU.add, accum_out=key_sum[:, :]))
                        nc.vector.tensor_tensor(key_col[:, :], key_sum[:, :], bqbk[:, :], ALU.add).then_inc(key_col_ready, 1)
                    if attend:
                        row_maximum(a, 6)
                        row_maximum(a, 7)
                    if chain:
                        for h in range(2):
                            dve.wait_ge(iscale_done, nth(2, c, h + 1))
                            nc.vector.tensor_tensor(tile4(xnT, h), tile4(xnT, h), shared[h][:, :], ALU.mult).then_inc(y_ready, 1)
                        for h in range(2):
                            dve.wait_ge(y_hi_ready, nth(2, c, h + 1))
                            dve.wait_ge(ffn_done, nth(2, c - 1, 2))
                            nc.vector.tensor_tensor(tile4(y_lo, h), tile4(xnT, h), tile4(y_hi, h).bitcast(F32),
                                                    ALU.subtract).then_inc(y_lo_ready, 1)
                        dve.wait_ge(biased, nth(1, c, 1))
                        half_of_x2(c, 0)
                    for s in range(T):
                        if attend:
                            dve.wait_ge(exp_ready, nth(8, a, s + 1))
                            dve.wait_ge(pv_done, nth(8, a, s - 1))
                            nc.vector.tensor_copy(p_hi[s % 2][:, :], prob[s % 2][:, :]).then_inc(p_hi_ready, 1)
                            dve.wait_ge(p_hi_ready, nth(8, a, s + 1))
                            nc.vector.tensor_tensor(p_lo[s % 2][:, :], prob[s % 2][:, :], p_hi[s % 2][:, :].bitcast(F32),
                                                    ALU.subtract).then_inc(p_lo_ready, 1)
                        if chain and s == 0:
                            half_of_x2(c, 1)
                        if chain and s == 1:
                            dve.wait_ge(x2_ready, nth(2, c, 2))
                            statistics(dve_chain, 2, c, res)
                        if chain and s == 3:
                            transposed_half(2, c)
                        if chain and s == 4:
                            dve.wait_ge(sc1_done, nth(1, c, 1))
                            nc.vector.tensor_reduce(r_max[1][:, :], shared[0][:, 0:P], AX_X, ALU.max,
                                                    negate=True).then_inc(s_max_ready, 1)
                        if chain and s == 6:
                            dve.wait_ge(attn_ready, nth(1, c, 1))
                            dve_chain.chain(dve, nc.vector.reciprocal(r_inv[1][:, :], r_sum[1][:, :]))
                    if chain:
                        for h in range(2):
                            dve.wait_ge(att_done, nth(2, c, h + 1))
                            nc.vector.scalar_tensor_tensor(res[:, half(h)], shared[h][:, :], r_inv[1][:, :], res[:, half(h)],
                                                           ALU.mult, ALU.add).then_inc(x3_ready, 1)
                        dve.wait_ge(x3_ready, nth(2, c, 2))
                        statistics(dve_chain, 3, c, res)
                    if attend:
                        dve.wait_ge(sc1_done, nth(1, a - 1, 1))
                        for h in range(2):
                            dve.wait_ge(kwT_done, nth(2, a, h + 1))
                            nc.vector.tensor_tensor(kwT[:, 4 * h:4 * h + 4, :], shared[h][:, :].rearrange("p (t c) -> p t c", t=4),
                                                    key_bias[:, 4 * h:4 * h + 4].unsqueeze(2).to_broadcast([P, 4, P]),
                                                    ALU.add).then_inc(kwT_ready, 1)
                    if prepare:
                        for h in range(2):
                            dve.wait_ge(q_hi_ready, nth(2, b, h + 1))
                            nc.vector.scalar_tensor_tensor(q_hl[DQK:P, half(h)], scores[0][DQK:P, half(h)], bq_col[DQK:P, :],
                                                           q_hl[DQK:P, half(h)].bitcast(F32), ALU.add,
                                                           ALU.subtract).then_inc(q_ready, 1)
                        dve.wait_ge(cT_done, nth(2, b, 2))
                        dve.wait_ge(kw_done, nth(2, b - 1, 2))
                        nc.vector.tensor_copy(tile4(cT, 1), shared[1][:, :]).then_inc(cT_b_ready, 1)
                        for h in range(2):
                            dve.wait_ge(k_hi_ready, nth(2, b, h + 1))
                            nc.vector.scalar_tensor_tensor(k_l1[0:DQK, half(h)], scores[1][0:DQK, half(h)], bk_col[0:DQK, :],
                                                           k_hh[0:DQK, half(h)].bitcast(F32), ALU.add,
                                                           ALU.subtract).then_inc(k_ready, 1)
                    if chain:
                        transposed_half(3, c)
                    if chain:
                        dve.wait_ge(low_done, nth(1, c, 1))
                        dve_chain.chain(dve, nc.vector.tensor_tensor(logit[:, :], shared[0][:, HR:HR + E], br_rows[:, :], ALU.add))
                        nc.vector.tensor_reduce(r_max[2][:, :], logit[:, :], AX_X, ALU.max, negate=True).then_inc(l_max_ready, 1)
                    if attend:
                        dve.wait_ge(den_done, nth(1, a, 1))
                        dve.wait_ge(den_turned, nth(2, a - 1, 2))
                        nc.vector.reciprocal(den_inv[:, :], shared[1][:, 0:T * T].rearrange("p (t e) -> p t e", t=T)[:, :, 0]
                                             ).then_inc(den_inv_ready, 1)
                    if chain:
                        dve.wait_ge(l_exp_ready, nth(1, c, 1))
                        dve_chain.chain(dve, nc.vector.reciprocal(r_inv[2][:, :], r_sum[2][:, :]))
                        dve_chain.chain(dve, nc.vector.tensor_scalar(route1[:, :], r_exp[1][:, :], r_inv[2][:, :], LORA, ALU.mult, ALU.mult))
                        dve.wait_ge(lowT_done, nth(1, c - 1, 1))
                        nc.vector.tensor_tensor(low[:, :].rearrange("p (h r) -> p h r", h=E),
                                                shared[0][:, 0:HR].rearrange("p (h r) -> p h r", h=E),
                                                route1[:, :].unsqueeze(2).to_broadcast([P, E, R]), ALU.mult).then_inc(low_ready, 1)
                    if prepare:
                        for h in range(2):
                            dve.wait_ge(v_hi_ready, nth(2, b, h + 1))
                            nc.vector.tensor_tensor(tile4(v_lo, h), scores[0][:, half(h)], tile4(v_hi, h).bitcast(F32),
                                                    ALU.subtract).then_inc(v_ready, 1)
                    if attend:
                        dve.wait_ge(pv_done, nth(8, a, 8))
                        dve.wait_ge(x1_loaded, nth(16, a, 16))
                        for h in range(2):
                            dve.wait_ge(den_rows_ready, nth(2, a, h + 1))
                            dve_attend.chain(dve, nc.vector.tensor_tensor(den_rows[:, half(h)], acc[:, half(h)], den_rows[:, half(h)], ALU.mult))
                            nc.vector.scalar_tensor_tensor(x1[:, half(h)], den_rows[:, half(h)], bv_col[:, :], x1[:, half(h)],
                                                           ALU.add, ALU.add).then_inc(x1_ready, 1)
                        dve.wait_ge(x1_ready, nth(2, a, 2))
                        statistics(dve_attend, 1, a, x1)
                        dve_attend.end()
                    if chain:
                        dve.wait_ge(stored, nth(16, c - 1, 16))
                        for h in range(2):
                            dve.wait_ge(out_done, nth(2, c, h + 1))
                            nc.vector.tensor_tensor(result[:, half(h)], shared[h][:, :], res[:, half(h)], ALU.add).then_inc(out_ready, 1)
                        dve_chain.end()

                iterations(dve, body)

            @block.tensor
            def _(pe):
                mm = nc.tensor.matmul
                pe.wait_ge(const_made, 3)

                def transposes(h, src, semaphore):
                    for j in range(4):
                        t = 4 * h + j
                        last = nc.tensor.transpose(shared[h][:, j * P:(j + 1) * P], src[:, t * P:(t + 1) * P], ident[:, :])
                    last.then_inc(semaphore, 1)

                def query_scores(a, t):
                    if t == 0:
                        pe.wait_ge(q_ready, nth(2, a, 2))
                        pe.wait_ge(k_ready, nth(2, a, 2))
                        pe.wait_ge(v_ready, nth(2, a, 2))
                    if t >= 2:
                        pe.wait_ge(row_max, nth(8, a, t - 1))
                    for h in range(2):
                        last = mm(scores[t % 2][:, half(h)], q_hl[:, t * P:(t + 1) * P], k_hh[:, half(h)], start=True, stop=True)
                    last.then_inc(maxscores_done, 1)

                def keys_through_queries(a, t):
                    h = t // 4
                    if t == 0:
                        pe.wait_ge(x1_ready, nth(2, a - 1, 2))
                        pe.wait_ge(cT_a_ready, nth(1, a, 1))
                        pe.wait_ge(cT_b_ready, nth(1, a, 1))
                    for f in (2 * (t % 4), 2 * (t % 4) + 1):
                        last = mm(acc[:, half(h)], cT[:, f, :], mT[:, f, half(h)], start=f == 0, stop=f == T - 1)
                    if f == T - 1:
                        last.then_inc(kw_done, 1)

                def feed_forward(h):
                    for f in range(T):
                        mm(shared[h][:, :], y_hi[:, f, :], signT[:, f, half(h)], start=f == 0, stop=False)
                        last = mm(shared[h][:, :], y_lo[:, f, :], signT[:, f, half(h)], start=False, stop=f == T - 1)
                    last.then_inc(ffn_done, 1)

                def key_scores(a, s):
                    if s == 0:
                        pe.wait_ge(max_ready, nth(2, a, 2))
                    elif s == 1:
                        pe.wait_ge(row_max, nth(8, a, 8))
                    else:
                        pe.wait_ge(exp_ready, nth(8, a, s - 1))
                    for h in range(2):
                        mm(scores[s % 2][:, half(h)], k_hh[:, s * P:(s + 1) * P], q_hl[:, half(h)], start=True, stop=False)
                        last = mm(scores[s % 2][:, half(h)], k_l1[:, s * P:(s + 1) * P], q_hm[:, half(h)], start=False, stop=True)
                    last.then_inc(scores_done, 1)

                def weigh_values(a, s):
                    if s == 0:
                        pe.wait_ge(kw_ready, nth(2, a, 2))
                        pe.wait_ge(v_ready, nth(2, a, 2))
                    pe.wait_ge(p_hi_ready, nth(8, a, s + 1))
                    pe.wait_ge(p_lo_ready, nth(8, a, s + 1))
                    for v, p, first, end in ((v_hi, p_hi, s == 0, False), (v_lo, p_hi, False, False), (v_hi, p_lo, False, s == T - 1)):
                        for h in range(2):
                            last = mm(acc[:, half(h)], v[:, s, :], p[s % 2][:, half(h)], start=first, stop=end)
                    last.then_inc(pv_done, 1)

                def body(k, prepare, attend, chain):
                    b, a, c = k, k - 1, k - 2
                    for t in range(T):
                        if attend:
                            query_scores(a, t)
                        if chain and t == 2:
                            pe.wait_ge(normed[1], nth(1, c, 1))
                            for h in range(2):
                                pe.wait_ge(out_ready, nth(2, c - 1, h + 1))
                                transposes(h, xn_c, xnT_done[1])
                        if chain and t == 4:
                            pe.wait_ge(xnT_a_ready[1], nth(1, c, 1))
                            pe.wait_ge(xnT_b_ready[1], nth(1, c, 1))
                            for f in range(T):
                                last = mm(shared[0][:, 0:E], xnT[:, f, :], gateT[:, f, 0:E], start=f == 0, stop=f == T - 1)
                            last.then_inc(route_done, 1)
                        if chain and t == 6:
                            pe.wait_ge(route_ready, nth(1, c, 1))
                            nc.tensor.transpose(shared[1][0:96, 0:P], route3[:, :].bitcast(F32), ident[:, :]).then_inc(routeT_done, 1)
                        if chain and t == 7:
                            pe.wait_ge(routeT_ready, nth(1, c, 1))
                            pe.wait_ge(r_exp_ready, nth(1, c, 1))
                            for h in range(2):
                                for j in range(4):
                                    f = 4 * h + j
                                    last = mm(shared[h][:, j * P:(j + 1) * P], ics3[:, f * P:(f + 1) * P], route3T[:, :],
                                              start=True, stop=True)
                                last.then_inc(iscale_done, 1)
                        if attend:
                            keys_through_queries(a, t)
                    if chain:
                        for h in range(2):
                            pe.wait_ge(y_ready, nth(2, c, h + 1))
                            mm(shared[h][:, :], route3T[:, :], ocs3[:, half(h)], start=True, stop=True).then_inc(oscale_done, 1)
                    if attend:
                        pe.wait_ge(row_max, nth(8, a, 8))
                        for h in range(2):
                            for j in range(4):
                                t = 4 * h + j
                                last = nc.tensor.transpose(scores[0][0:DQK + 1, t * P:(t + 1) * P], neg_max[:, t:t + DQK + 1],
                                                           ident[:, :])
                            last.then_inc(max_turned, 1)
                    if chain:
                        pe.wait_ge(y_lo_ready, nth(2, c, 2))
                        pe.wait_ge(y_hi_ready, nth(2, c, 2))
                        pe.wait_ge(oscale_ready, nth(2, c, 1))
                        feed_forward(0)
                    if attend:
                        key_scores(a, 0)
                        key_scores(a, 1)
                    if chain:
                        pe.wait_ge(oscale_ready, nth(2, c, 2))
                        feed_forward(1)
                    for s in range(T):
                        if attend and s + 2 < T:
                            key_scores(a, s + 2)
                        if chain and s == 3:
                            pe.wait_ge(normed[2], nth(1, c, 1))
                            for h in range(2):
                                transposes(h, xn_c, xnT_done[2])
                        if chain and s == 4:
                            pe.wait_ge(xnT_a_ready[2], nth(1, c, 1))
                            pe.wait_ge(xnT_b_ready[2], nth(1, c, 1))
                            pe.wait_ge(kwT_ready, nth(2, c, 2))
                            pe.wait_ge(key_col_ready, nth(1, c, 1))
                            for f in range(T):
                                mm(shared[0][:, 0:P], xnT[:, f, :], kwT[:, f, :], start=f == 0, stop=False)
                            mm(shared[0][:, 0:P], key_col[:, :].to_broadcast([P, P]), ident[:, :], start=False,
                               stop=True).then_inc(sc1_done, 1)
                        if chain and s == 6:
                            pe.wait_ge(attn_ready, nth(1, c, 1))
                            nc.tensor.transpose(shared[1][:, 0:P], attn[:, :], ident[:, :]).then_inc(attnT_done, 1)
                        if prepare and s == 7:
                            pe.wait_ge(c_loaded, nth(16, b, 16))
                            pe.wait_ge(exp_ready, nth(8, a, 7))
                            for h in range(2):
                                mm(scores[0][:, half(h)], wqT[:, :], c_in[:, half(h)], start=True, stop=True).then_inc(q_done, 1)
                        if chain and s == 7:
                            pe.wait_ge(attnT_ready, nth(1, c, 1))
                            pe.wait_ge(val_loaded, nth(16, c, 16))
                            for h in range(2):
                                mm(shared[h][:, :], attnT[:, :], c_val[:, half(h)], start=True, stop=True).then_inc(att_done, 1)
                        if attend:
                            weigh_values(a, s)
                    if attend:
                        pe.wait_ge(kw_ready, nth(2, a, 2))
                        for h in range(2):
                            pe.wait_ge(x3_ready, nth(2, c, h + 1))
                            transposes(h, kw, kwT_done)
                    if prepare:
                        for h in range(2):
                            pe.wait_ge(kwT_ready, nth(2, a, h + 1))
                            transposes(h, c_in, cT_done)
                        pe.wait_ge(exp_ready, nth(8, a, 8))
                        for h in range(2):
                            mm(scores[1][:, half(h)], wkT[:, :], c_in[:, half(h)], start=True, stop=True).then_inc(k_done, 1)
                    if chain:
                        pe.wait_ge(normed[3], nth(1, c, 1))
                        for h in range(2):
                            pe.wait_ge(kwT_ready, nth(2, a, h + 1))
                            pe.wait_ge((cT_a_ready, cT_b_ready)[h], nth(1, b, 1))
                            transposes(h, xn_c, xnT_done[3])
                    if chain:
                        pe.wait_ge(xnT_a_ready[3], nth(1, c, 1))
                        pe.wait_ge(xnT_b_ready[3], nth(1, c, 1))
                        for f in range(T):
                            last = mm(shared[0][:, 0:HR + E], xnT[:, f, :], lowT[:, f, :], start=f == 0, stop=f == T - 1)
                        last.then_inc(low_done, 1)
                    if attend:
                        pe.wait_ge(p_summed, nth(7, a, 7))
                        pe.wait_ge(cT_b_ready, nth(1, b, 1))
                        for t in range(T):
                            last = mm(shared[1][:, t * T:(t + 1) * T], p_sum[:, t * P:(t + 1) * P], ones[:, :], start=True, stop=True)
                        last.then_inc(den_done, 1)
                    if prepare:
                        pe.wait_ge(normed[0], nth(1, b, 1))
                        pe.wait_ge(q_ready, nth(2, b, 2))
                        for h in range(2):
                            for j in range(4):
                                t = 4 * h + j
                                last = mm(scores[0][:, t * P:(t + 1) * P], xn[:, t * P:(t + 1) * P], wvT[:, :], start=True, stop=True)
                            last.then_inc(v_done, 1)
                    if chain:
                        pe.wait_ge(low_ready, nth(1, c, 1))
                        pe.wait_ge(den_inv_ready, nth(1, a, 1))
                        nc.tensor.transpose(shared[1][:, 0:P], low[:, :], ident[:, :]).then_inc(lowT_done, 1)
                    if attend:
                        pe.wait_ge(den_inv_ready, nth(1, a, 1))
                        pe.wait_ge(cT_a_ready, nth(1, b, 1))
                        for h in range(2):
                            if h == 1:
                                pe.wait_ge(lowT_ready, nth(1, c, 1))
                            for j in range(4):
                                t = 4 * h + j
                                last = nc.tensor.transpose(shared[h][:, j * P:(j + 1) * P],
                                                           den_inv[:, t:t + 1].to_broadcast([P, P]), ident[:, :])
                            last.then_inc(den_turned, 1)
                    if chain:
                        pe.wait_ge(lowT_ready, nth(1, c, 1))
                        for h in range(2):
                            pe.wait_ge(den_rows_ready, nth(2, a, h + 1))
                            mm(shared[h][:, :], low_T[:, :], bT[:, half(h)], start=True, stop=True).then_inc(out_done, 1)

                iterations(pe, body)


_INS = ['x', 'ctx_4096', 'L0_xattn_Wq', 'L0_xattn_bq', 'L0_xattn_Wk', 'L0_xattn_bk', 'L0_xattn_Wv', 'L0_xattn_bv',
        'L0_ffn_weight', 'L0_ffn_bias', 'L0_ffn_gate_w', 'L0_ffn_in_channel_scale', 'L0_ffn_out_channel_scale',
        'L1_xattn_Wq', 'L1_xattn_bq', 'L1_xattn_Wk', 'L1_xattn_bk', 'L1_ffn_A', 'L1_ffn_B', 'L1_ffn_Wr', 'L1_ffn_br']


def kernel(**inputs):
    import numpy as np
    import concourse.bacc as bacc
    from concourse import mybir
    from concourse.bass_utils import run_bass_kernel_spmd

    nc = bacc.Bacc("TRN2", target_bir_lowering=False, num_devices=1)
    arrays, args = {}, []
    for name in _INS:
        a = np.ascontiguousarray(inputs[name])
        arrays[f"in_{name}"] = a
        args.append(nc.dram_tensor(f"in_{name}", a.shape, mybir.dt.from_np(a.dtype), kind="ExternalInput").ap())
    args.append(nc.dram_tensor("out_x", inputs["x"].shape, mybir.dt.float32, kind="ExternalOutput").ap())
    build(nc, *args)
    return run_bass_kernel_spmd(nc, [arrays], core_ids=[0]).results[0]["out_x"]
```

```python
from contextlib import ExitStack

import concourse.bass as bass
from concourse import mybir

F32 = mybir.dt.float32
F32R = mybir.dt.float32r
ALU = mybir.AluOpType
ACT = mybir.ActivationFunctionType
AX_X = mybir.AxisListType.X

P = 128
HALF = 512
EPS = 1e-5


class Steps:

    def __init__(self, sem, per):
        self.sem, self.per = sem, per

    def begin(self, b):
        self.base, self.n = b * self.per, 0

    def chain(self, engine, instruction):
        self.n += 1
        instruction.then_inc(self.sem, 1)
        engine.wait_ge(self.sem, self.base + self.n)

    def end(self):
        assert self.n == self.per, (self.n, self.per)


def build(nc, x, ctx_, wq0, bq0, wk0, bk0, wv0, bv0, w_ffn, b_ffn, gate, ics, ocs,
          wq1, bq1, wk1, bk1, a1, b1, wr1, br1, out):
    NB, S, D = x.shape
    DQK = wq0.shape[0]
    E = gate.shape[0]
    R = a1.shape[1]
    HR = E * R
    T = D // P
    SCALE1 = float(D) ** -0.5
    LORA = 2.0 * E
    assert S == P and HR == P and 2 * DQK == P and D == 2 * HALF

    top = ExitStack()
    with top:
        def sb(name, shape, dt=F32, stack=top):
            return stack.enter_context(nc.sbuf_tensor(name, shape, dt))

        def sem(name, stack=top):
            return stack.enter_context(nc.semaphore(name))

        ident = sb("ident", [P, P])
        ones = sb("ones", [P, T])
        minus_half = sb("minus_half", [P, 1])
        wqT = sb("wqT", [P, P])
        wkT = sb("wkT", [P, P])
        wvT = sb("wvT", [P, P])
        bq_col = sb("bq_col", [P, 1])
        bk_col = sb("bk_col", [P, 1])
        bv_col = sb("bv_col", [P, 1])
        signT = sb("signT", [P, T, D], F32R)
        gateT = sb("gateT", [P, T, 2 * E])
        ics3 = sb("ics3", [96, D], F32R)
        ocs3 = sb("ocs3", [96, D], F32R)
        bias_rows = sb("bias_rows", [P, D])
        mT = sb("mT", [P, T, D])
        key_bias = sb("key_bias", [P, T])
        query_bias = sb("query_bias", [P, D])
        bqbk = sb("bqbk", [P, 1])
        lowT = sb("lowT", [P, T, HR + E])
        bT = sb("bT", [P, D])
        br_rows = sb("br_rows", [P, E])

        with ExitStack() as tmp:
            with ExitStack() as whole:
                wq_nat = sb("wq_nat", [P, T, D], F32, whole)
                wk_nat = sb("wk_nat", [P, T, D], F32, whole)
                a_nat = sb("a_nat", [P, T, P], F32, whole)
                b_nat = sb("b_nat", [P, T, P], F32, whole)
            wq_lo = sb("wq_lo", [P, T, D], F32R, tmp)
            wk_lo = sb("wk_lo", [P, T, D], F32R, tmp)
            wk_hi = [sb(f"wk_hi{i}", [P, T, P], F32R, tmp) for i in range(2)]
            wq_hi = sb("wq_hi", [P, T, D], F32R, tmp)
            bq_parts = sb("bq_parts", [P, T, 2], F32R, tmp)
            bk_parts = sb("bk_parts", [P, T, 2], F32R, tmp)
            bq_first = sb("bq_first", [P, T, 2], F32R, tmp)
            bk_first = sb("bk_first", [P, T, 2], F32R, tmp)
            wf_nat = mT
            small = sb("small", [P, 3, P], F32, tmp)
            g_nat = sb("g_nat", [2 * E, D], F32, tmp)
            bq1_col = sb("bq1_col", [P, T], F32, tmp)
            bk1_col = sb("bk1_col", [P, T], F32, tmp)
            ics_f = query_bias[0:96, :]
            ocs_f = sb("ocs_f", [96, D], F32, tmp)
            bk_rows = ocs_f[0:2, :]
            bq_rows = query_bias[0:2, :]
            bank = [tmp.enter_context(nc.psum_tensor(f"setup{i}", [P, HALF], F32)) for i in range(8)]
            zeroed = sem("zeroed", tmp)
            ident_made = sem("ident_made", tmp)
            ones_made = sem("ones_made", tmp)
            small_in = sem("small_in", tmp)
            scales_in = sem("scales_in", tmp)
            low_in = sem("low_in", tmp)
            bias_in = sem("bias_in", tmp)
            wf_in = [sem(f"wf_in{i}", tmp) for i in range(2)]
            wq_in = [sem(f"wq_in{i}", tmp) for i in range(4)]
            wk_in = [sem(f"wk_in{i}", tmp) for i in range(T)]
            filled = sem("filled", tmp)
            signed = sem("signed", tmp)
            copied = sem("copied", tmp)
            split = sem("split", tmp)
            bias_split = sem("bias_split", tmp)
            wq_hi_made = sem("wq_hi_made", tmp)
            wq_lo_made = sem("wq_lo_made", tmp)
            wk_hi_made = sem("wk_hi_made", tmp)
            wk_lo_made = sem("wk_lo_made", tmp)

            groups = ([("sign", i) for i in range(T)] + [("low", 0), ("low", 1), ("b", 0), ("b", 1)]
                      + [("sign", i) for i in range(T, 2 * T)])
            for ft in range(T):
                groups += [("m", 2 * ft), ("m", 2 * ft + 1), ("bq_rows", ft)]
                if ft == 1:
                    groups += [("small", 0), ("gate", 0), ("bk_rows", 0), ("bk_rows", 1), ("bk_col", 0)]
            groups += [("query_bias", 0), ("query_bias", 1)]

            with nc.Block() as block:
                @block.sync
                def _(sp):
                    for i in range(4):
                        sp.dma_start(wq_nat[:, 2 * i:2 * i + 2, :],
                                     wq1[2 * i * P:(2 * i + 2) * P, :].rearrange("(t p) x -> p t x", p=P)).then_inc(wq_in[i], 16)
                    for i in range(2):
                        sp.dma_start(wf_nat[:, 4 * i:4 * i + 4, :],
                                     w_ffn[4 * i * P:(4 * i + 4) * P, :].rearrange("(t p) h -> p t h", p=P)).then_inc(wf_in[i], 16)
                    for i in range(T):
                        sp.dma_start(wk_nat[:, :, i * P:(i + 1) * P],
                                     wk1[:, i * P:(i + 1) * P].rearrange("(t p) f -> p t f", p=P)).then_inc(wk_in[i], 16)

                @block.gpsimd
                def _(pool):
                    nc.gpsimd.memset(ident[:, :], 0.0).then_inc(ident_made, 1)
                    pool.wait_ge(ident_made, 1)
                    nc.gpsimd.affine_select(out=ident[:, :], in_=ident[:, :], compare_op=ALU.not_equal, fill=1.0,
                                            base=0, pattern=[[-1, P]], channel_multiplier=1).then_inc(ident_made, 1)
                    nc.gpsimd.memset(ones[:, :], 1.0).then_inc(ones_made, 1)
                    nc.gpsimd.memset(minus_half[:, :], -0.5)

                @block.scalar
                def _(act):
                    act.dma_start(a_nat[:, :, :].rearrange("p t d -> p (t d)"),
                                  a1.rearrange("h r d -> (h r) d")).then_inc(low_in, 16)
                    for h in range(E):
                        act.dma_start(b_nat[:, :, h * R:(h + 1) * R],
                                      b1[h].rearrange("(t p) r -> p t r", p=P)).then_inc(low_in, 16)
                    act.dma_start(bq1_col[:, :], bq1.rearrange("(t p) -> p t", p=P), allow_slow_non_contiguous=True).then_inc(bias_in, 16)
                    act.dma_start(bk1_col[:, :], bk1.rearrange("(t p) -> p t", p=P), allow_slow_non_contiguous=True).then_inc(bias_in, 16)
                    n_small = 0
                    for dst, src in (
                        (small[0:DQK, 0, :], wq0), (small[DQK:P, 0, :], wq0),
                        (small[0:DQK, 1, :], wk0), (small[DQK:P, 1, :], wk0), (small[:, 2, :], wv0),
                        (bq_col[0:DQK, :], bq0.unsqueeze(1)), (bq_col[DQK:P, :], bq0.unsqueeze(1)),
                        (bk_col[0:DQK, :], bk0.unsqueeze(1)), (bk_col[DQK:P, :], bk0.unsqueeze(1)),
                        (bv_col[:, :], bv0.unsqueeze(1)),
                        (g_nat[0:E, :], gate), (g_nat[E:2 * E, :], wr1),
                        (bias_rows[:, :], b_ffn.partition_broadcast(P)),
                        (br_rows[:, :], br1.partition_broadcast(P)),
                    ):
                        act.dma_start(dst, src).then_inc(small_in, 16)
                        n_small += 1
                    assert n_small == 14
                    act.wait_ge(zeroed, 2)
                    for k in range(3):
                        act.dma_start(ics_f[32 * k:32 * k + E, :], ics).then_inc(scales_in, 16)
                        act.dma_start(ocs_f[32 * k:32 * k + E, :], ocs).then_inc(scales_in, 16)
                    for t in range(T):
                        act.wait_ge(wq_in[t // 2], 16)
                        nc.scalar.activation(wq_hi[:, t, :], wq_nat[:, t, :], ACT.Identity).then_inc(wq_hi_made, 1)
                    for n, (kind, i) in enumerate(groups):
                        if kind != "sign":
                            continue
                        act.wait_ge(filled, n + 1)
                        nc.scalar.activation(signT[:, i % T, (i // T) * HALF:(i // T + 1) * HALF], bank[n % 8][:, :],
                                             ACT.Sign).then_inc(signed, 1)

                @block.vector
                def _(dve):
                    def split_keys(ft):
                        cols = slice(ft * P, (ft + 1) * P)
                        dve.wait_ge(wk_in[ft], 16)
                        nc.vector.tensor_copy(wk_hi[ft % 2][:, :, :], wk_nat[:, :, cols]).then_inc(wk_hi_made, 1)
                        dve.wait_ge(wk_hi_made, ft + 1)
                        nc.vector.tensor_tensor(wk_lo[:, :, cols], wk_nat[:, :, cols],
                                                wk_hi[ft % 2][:, :, :].bitcast(F32), ALU.subtract).then_inc(wk_lo_made, 1)

                    nc.vector.memset(ics_f, 0.0).then_inc(zeroed, 1)
                    nc.vector.memset(ocs_f[:, :], 0.0).then_inc(zeroed, 1)
                    nc.vector.memset(bq_first[:, :, :].bitcast(F32), 0.0).then_inc(zeroed, 1)
                    nc.vector.memset(bk_first[:, :, :].bitcast(F32), 0.0).then_inc(zeroed, 1)
                    for t in range(T):
                        dve.wait_ge(wq_hi_made, t + 1)
                        nc.vector.tensor_tensor(wq_lo[:, t, :], wq_nat[:, t, :], wq_hi[:, t, :].bitcast(F32),
                                                ALU.subtract).then_inc(wq_lo_made, 1)
                    for n, (kind, i) in enumerate(groups):
                        if kind == "sign":
                            continue
                        if (kind, i) == ("m", 0):
                            dve.wait_ge(bias_in, 2 * 16)
                            dve.wait_ge(zeroed, 4)
                            for parts, first, full in ((bq_parts, bq_first, bq1_col), (bk_parts, bk_first, bk1_col)):
                                nc.vector.tensor_copy(parts[:, :, 0], full[:, :]).then_inc(bias_split, 1)
                                nc.vector.tensor_copy(first[:, :, 0], full[:, :]).then_inc(bias_split, 1)
                            dve.wait_ge(bias_split, 4)
                            for parts, full in ((bq_parts, bq1_col), (bk_parts, bk1_col)):
                                nc.vector.tensor_tensor(parts[:, :, 1], full[:, :], parts[:, :, 0].bitcast(F32),
                                                        ALU.subtract).then_inc(bias_split, 1)
                        if (kind, i) == ("bq_rows", 0):
                            dve.wait_ge(scales_in, 6 * 16)
                            nc.vector.tensor_copy(ics3[:, :], ics_f).then_inc(split, 1)
                            nc.vector.tensor_copy(ocs3[:, :], ocs_f[:, :]).then_inc(split, 1)
                            dve.wait_ge(split, 2)
                            for hi, full in ((ics3, query_bias), (ocs3, ocs_f)):
                                nc.vector.tensor_tensor(hi[64:96, :], full[64:96, :], hi[64:96, :].bitcast(F32), ALU.subtract).then_inc(split, 1)
                            dve.wait_ge(split, 4)
                        dve.wait_ge(filled, n + 1)
                        s = bank[n % 8]
                        if kind == "small":
                            nc.vector.tensor_copy(wqT[:, :], s[:, 0:P])
                            nc.vector.tensor_copy(wkT[:, :], s[:, P:2 * P])
                            last = nc.vector.tensor_copy(wvT[:, :], s[:, 2 * P:3 * P])
                        elif kind == "gate":
                            nc.vector.tensor_copy(gateT[:, :, :], s[:, 0:T * 2 * E].rearrange("p (t e) -> p t e", t=T))
                            last = nc.vector.tensor_copy(
                                lowT[:, :, HR:HR + E], s[:, 0:T * 2 * E].rearrange("p (t e) -> p t e", t=T)[:, :, E:2 * E])
                        elif kind == "low":
                            last = nc.vector.tensor_copy(lowT[:, 4 * i:4 * i + 4, 0:HR],
                                                         s[:, :].rearrange("p (t e) -> p t e", t=4))
                        elif kind == "b":
                            last = nc.vector.tensor_copy(bT[:, i * HALF:(i + 1) * HALF], s[:, :])
                        elif kind == "bk_rows":
                            last = nc.vector.tensor_copy(bk_rows[:, i * HALF:(i + 1) * HALF], s[0:2, :])
                        elif kind == "bk_col":
                            nc.vector.tensor_copy(key_bias[:, :], s[:, 0:T])
                            last = nc.vector.tensor_copy(bqbk[:, :], s[:, T:T + 1])
                        elif kind == "m":
                            last = nc.vector.tensor_copy(mT[:, i // 2, (i % 2) * HALF:(i % 2 + 1) * HALF], s[:, :])
                        elif kind == "bq_rows":
                            last = nc.vector.tensor_copy(bq_rows[:, i * P:(i + 1) * P], s[0:2, 0:P])
                        else:
                            last = nc.vector.tensor_copy(query_bias[:, i * HALF:(i + 1) * HALF], s[:, :])
                        last.then_inc(copied, 1)
                        if kind == "b" and i == 1:
                            split_keys(0)
                            split_keys(1)
                        if kind == "bq_rows" and i + 2 < T:
                            split_keys(i + 2)

                @block.tensor
                def _(pe):
                    mm = nc.tensor.matmul
                    pe.wait_ge(ident_made, 2)
                    for n, (kind, i) in enumerate(groups):
                        if n >= 8:
                            by_act = groups[n - 8][0] == "sign"
                            pe.wait_ge(signed if by_act else copied,
                                       sum((g[0] == "sign") == by_act for g in groups[:n - 7]))
                        s = bank[n % 8]
                        if kind == "small":
                            pe.wait_ge(small_in, 14 * 16)
                            for j in range(3):
                                last = nc.tensor.transpose(s[:, j * P:(j + 1) * P], small[:, j, :], ident[:, :])
                        elif kind == "gate":
                            for t in range(T):
                                last = nc.tensor.transpose(s[:, t * 2 * E:(t + 1) * 2 * E], g_nat[:, t * P:(t + 1) * P],
                                                           ident[0:2 * E, 0:2 * E])
                        elif kind in ("low", "b"):
                            if kind == "low" and i == 0:
                                pe.wait_ge(low_in, 16 * (1 + E))
                            for j in range(4):
                                src = a_nat if kind == "low" else b_nat
                                last = nc.tensor.transpose(s[:, j * P:(j + 1) * P], src[:, 4 * i + j, :], ident[:, :])
                        elif kind == "sign":
                            if i % T == 0:
                                pe.wait_ge(wf_in[i // T], 16)
                            for j in range(4):
                                last = nc.tensor.transpose(s[:, j * P:(j + 1) * P],
                                                           wf_nat[:, 4 * (i // T) + j, (i % T) * P:(i % T + 1) * P], ident[:, :])
                        elif kind == "bk_rows":
                            if i == 0:
                                pe.wait_ge(bias_split, 6)
                                pe.wait_ge(wq_hi_made, T)
                                pe.wait_ge(wq_lo_made, T)
                            for t in range(T):
                                mm(s[0:2, :], bk_parts[:, t, :], wq_hi[:, t, i * HALF:(i + 1) * HALF], start=t == 0, stop=False)
                                last = mm(s[0:2, :], bk_first[:, t, :], wq_lo[:, t, i * HALF:(i + 1) * HALF], start=False, stop=t == T - 1)
                        elif kind == "bk_col":
                            pe.wait_ge(ones_made, 1)
                            pe.wait_ge(copied, sum(g[0] != "sign" for g in groups[:n]))
                            for j in range(T):
                                mm(s[:, j:j + 1], bk_rows[:, j * P:(j + 1) * P], ones[0:2, 0:1], start=True, stop=True)
                            for t in range(T):
                                last = mm(s[:, T:T + 1], bq1_col[:, t:t + 1].to_broadcast([P, P]), bk1_col[:, t:t + 1],
                                          start=t == 0, stop=t == T - 1)
                        elif kind == "m":
                            ft, cols = i // 2, slice((i % 2) * HALF, (i % 2 + 1) * HALF)
                            if i % 2 == 0:
                                pe.wait_ge(wq_hi_made, T)
                                pe.wait_ge(wq_lo_made, T)
                                pe.wait_ge(wk_hi_made, ft + 1)
                                pe.wait_ge(wk_lo_made, ft + 1)
                            for t in range(T):
                                mm(s[:, :], wk_hi[ft % 2][:, t, :], wq_hi[:, t, cols], start=t == 0, stop=False)
                                mm(s[:, :], wk_hi[ft % 2][:, t, :], wq_lo[:, t, cols], start=False, stop=False)
                                last = mm(s[:, :], wk_lo[:, t, ft * P:(ft + 1) * P], wq_hi[:, t, cols], start=False, stop=t == T - 1)
                        elif kind == "bq_rows":
                            pe.wait_ge(bias_split, 6)
                            for t in range(T):
                                mm(s[0:2, 0:P], bq_parts[:, t, :], wk_hi[i % 2][:, t, :], start=t == 0, stop=False)
                                last = mm(s[0:2, 0:P], bq_first[:, t, :], wk_lo[:, t, i * P:(i + 1) * P], start=False, stop=t == T - 1)
                        else:
                            pe.wait_ge(copied, sum(g[0] != "sign" for g in groups[:n - i]))
                            last = mm(s[:, :], ones[0:2, 0:1].to_broadcast([2, P]), bq_rows[:, i * HALF:(i + 1) * HALF],
                                      start=True, stop=True)
                        last.then_inc(filled, 1)

        c_in = sb("c_in", [P, D])
        xn = sb("xn", [P, D])
        v_hi = sb("v_hi", [P, T, P], F32R)
        v_lo = sb("v_lo", [P, T, P], F32R)
        q_hl = sb("q_hl", [P, D], F32R)
        q_hm = sb("q_hm", [DQK + 1, D], F32R)
        k_hh = sb("k_hh", [P, D], F32R)
        k_l1 = sb("k_l1", [DQK + 1, D], F32R)
        cT = sb("cT", [P, T, P])
        neg_max = sb("neg_max", [P, DQK + T])
        prob = [sb(f"prob{i}", [P, D]) for i in range(2)]
        p_hi = [sb(f"p_hi{i}", [P, D], F32R) for i in range(2)]
        p_lo = [sb(f"p_lo{i}", [P, D], F32R) for i in range(2)]
        p_sum = sb("p_sum", [P, D])
        x1 = sb("x1", [P, D])
        kw = sb("kw", [P, D])
        kwT = sb("kwT", [P, T, P])
        den_inv = sb("den_inv", [P, T])
        den_rows = sb("den_rows", [P, D])
        res = sb("res", [P, D])
        xn_c = sb("xn_c", [P, D])
        xnT = sb("xnT", [P, T, P])
        y_hi = sb("y_hi", [P, T, P], F32R)
        y_lo = sb("y_lo", [P, T, P], F32R)
        oscale = sb("oscale", [P, D])
        c_val = sb("c_val", [P, D])
        stat = [sb(f"stat{i}", [P, 12]) for i in range(4)]
        mean_var = [sb(f"mean_var{i}", [P, 2]) for i in range(4)]
        neg_mean = [sb(f"neg_mean{i}", [P, 1]) for i in range(4)]
        var_eps = [sb(f"var_eps{i}", [P, 1]) for i in range(4)]
        rstd = [sb(f"rstd{i}", [P, 1]) for i in range(4)]
        shift = [sb(f"shift{i}", [P, 1]) for i in range(4)]
        logit = sb("logit", [P, E])
        r_max = [sb(f"r_max{i}", [P, 1]) for i in range(3)]
        r_bias = sb("r_bias", [P, 1])
        r_exp = [sb(f"r_exp{i}", [P, E]) for i in range(2)]
        r_sum = [sb(f"r_sum{i}", [P, 1]) for i in range(3)]
        r_inv = [sb(f"r_inv{i}", [P, 1]) for i in range(3)]
        route = sb("route", [P, E])
        route1 = sb("route1", [P, E])
        route3 = sb("route3", [P, 96], F32R)
        route3T = sb("route3T", [96, P], F32R)
        key_sum = sb("key_sum", [P, 1])
        key_col = sb("key_col", [P, 1])
        result = sb("result", [P, D])
        attn = sb("attn", [P, P])
        attnT = sb("attnT", [P, P])
        low = sb("low", [P, HR])
        low_T = sb("low_T", [P, P])

        def psum(name, shape):
            return top.enter_context(nc.psum_tensor(name, shape, F32))

        scores = [psum(f"scores{i}", [P, D]) for i in range(2)]
        acc = psum("acc", [P, D])
        shared = [psum(f"shared{i}", [P, HALF]) for i in range(2)]

        const_made = sem("const_made")
        c_loaded = sem("c_loaded")
        xn_loaded = sem("xn_loaded")
        x1_loaded = sem("x1_loaded")
        val_loaded = sem("val_loaded")
        stored = sem("stored")
        var_ready = [sem(f"var_ready{i}") for i in range(4)]
        shift_ready = [sem(f"shift_ready{i}") for i in range(4)]
        normed = [sem(f"normed{i}") for i in range(4)]
        cT_done = sem("cT_done")
        q_done = sem("q_done")
        k_done = sem("k_done")
        v_done = sem("v_done")
        maxscores_done = sem("maxscores_done")
        kw_done = sem("kw_done")
        max_turned = sem("max_turned")
        scores_done = sem("scores_done")
        pv_done = sem("pv_done")
        den_done = sem("den_done")
        den_turned = sem("den_turned")
        kwT_done = sem("kwT_done")
        xnT_done = [None] + [sem(f"xnT_done{i}") for i in (1, 2, 3)]
        route_done = sem("route_done")
        routeT_done = sem("routeT_done")
        iscale_done = sem("iscale_done")
        oscale_done = sem("oscale_done")
        ffn_done = sem("ffn_done")
        sc1_done = sem("sc1_done")
        attnT_done = sem("attnT_done")
        att_done = sem("att_done")
        low_done = sem("low_done")
        lowT_done = sem("lowT_done")
        out_done = sem("out_done")
        cT_a_ready = sem("cT_a_ready")
        cT_b_ready = sem("cT_b_ready")
        k_hi_ready = sem("k_hi_ready")
        q_hi_ready = sem("q_hi_ready")
        q_ready = sem("q_ready")
        k_ready = sem("k_ready")
        v_hi_ready = sem("v_hi_ready")
        v_ready = sem("v_ready")
        row_max = sem("row_max")
        kw_ready = sem("kw_ready")
        max_ready = sem("max_ready")
        exp_ready = sem("exp_ready")
        p_hi_ready = sem("p_hi_ready")
        p_lo_ready = sem("p_lo_ready")
        p_summed = sem("p_summed")
        den_inv_ready = sem("den_inv_ready")
        den_rows_ready = sem("den_rows_ready")
        x1_ready = sem("x1_ready")
        kwT_ready = sem("kwT_ready")
        key_col_ready = sem("key_col_ready")
        xnT_a_ready = [None] + [sem(f"xnT_a_ready{i}") for i in (1, 2, 3)]
        xnT_b_ready = [None] + [sem(f"xnT_b_ready{i}") for i in (1, 2, 3)]
        biased = sem("biased")
        r_max_ready = sem("r_max_ready")
        r_exp_ready = sem("r_exp_ready")
        route_ready = sem("route_ready")
        routeT_ready = sem("routeT_ready")
        y_ready = sem("y_ready")
        y_hi_ready = sem("y_hi_ready")
        y_lo_ready = sem("y_lo_ready")
        oscale_ready = sem("oscale_ready")
        x2_ready = sem("x2_ready")
        s_max_ready = sem("s_max_ready")
        attn_ready = sem("attn_ready")
        attnT_ready = sem("attnT_ready")
        x3_ready = sem("x3_ready")
        l_max_ready = sem("l_max_ready")
        l_exp_ready = sem("l_exp_ready")
        low_ready = sem("low_ready")
        lowT_ready = sem("lowT_ready")
        out_ready = sem("out_ready")
        dve_prepare = Steps(sem("dve_prepare"), 2)
        dve_attend = Steps(sem("dve_attend"), 4)
        dve_chain = Steps(sem("dve_chain"), 14)
        pool_norm = [Steps(sem(f"pool_norm{i}"), 1) for i in range(4)]
        act_chain = Steps(sem("act_chain"), 1)

        KW_UNITS = (3, 4, 6, 7, 9, 11, 12, 14, 16)

        def half(h):
            return slice(h * HALF, (h + 1) * HALF)

        def tile4(buf, h):
            return buf[:, 4 * h:4 * h + 4, :].rearrange("p t c -> p (t c)")

        def nth(per, b, n):
            if isinstance(b, int):
                return max(0, per * min(b, NB - 1) + n)
            return b * per + n

        def iterations(engine, body):
            for k in range(3):
                body(k, True, k >= 1, k >= 2)
            with engine.Fori(3, NB) as k:
                body(k, True, True, True)
            body(NB, False, True, True)
            body(NB + 1, False, False, True)

        with nc.Block() as block:

            @block.sync
            def _(sp):
                def body(k, prepare, attend, chain):
                    b, a, c = k, k - 1, k - 2
                    if chain:
                        sp.wait_ge(att_done, nth(2, c - 1, 2))
                        sp.dma_start(c_val[:, :], ctx_[c]).then_inc(val_loaded, 16)
                    if prepare:
                        sp.wait_ge(k_done, nth(2, b - 1, 2))
                        sp.dma_start(c_in[:, :], ctx_[b]).then_inc(c_loaded, 16)
                        sp.wait_ge(v_done, nth(2, b - 1, 2))
                        sp.dma_start(xn[:, :], x[b]).then_inc(xn_loaded, 16)
                    if attend:
                        sp.wait_ge(normed[1], nth(1, a - 1, 1))
                        sp.wait_ge(biased, nth(1, a - 1, 1))
                        sp.dma_start(x1[:, :], x[a]).then_inc(x1_loaded, 16)
                    if chain:
                        sp.wait_ge(out_ready, nth(2, c, 2))
                        sp.dma_start(out[c], result[:, :]).then_inc(stored, 16)

                iterations(sp, body)
                sp.wait_ge(stored, 16 * NB)

            @block.gpsimd
            def _(pool):
                def norm_scale(i, b):
                    pool.wait_ge(var_ready[i], nth(1, b, 1))
                    pool.wait_ge(normed[i], nth(1, b - 1, 1))
                    pool_norm[i].begin(b)
                    pool_norm[i].chain(pool, nc.gpsimd.tensor_tensor(rstd[i][:, :], var_eps[i][:, :], minus_half[:, :], ALU.pow))
                    nc.gpsimd.tensor_tensor(shift[i][:, :], neg_mean[i][:, :], rstd[i][:, :], ALU.mult).then_inc(shift_ready[i], 1)
                    pool_norm[i].end()

                def body(k, prepare, attend, chain):
                    b, a, c = k, k - 1, k - 2
                    if chain:
                        pool.wait_ge(x1_ready, nth(2, c, 2))
                        pool.wait_ge(out_ready, nth(2, c - 1, 2))
                        nc.gpsimd.tensor_tensor(res[:, :], x1[:, :], bias_rows[:, :], ALU.add).then_inc(biased, 1)
                    for s in range(T):
                        if attend and s >= 1:
                            pool.wait_ge(exp_ready, nth(8, a, s + 1))
                            if s == 1:
                                pool.wait_ge(den_done, nth(1, a - 1, 1))
                                nc.gpsimd.tensor_tensor(p_sum[:, :], prob[0][:, :], prob[1][:, :], ALU.add).then_inc(p_summed, 1)
                            else:
                                pool.wait_ge(p_summed, nth(7, a, s - 1))
                                nc.gpsimd.tensor_tensor(p_sum[:, :], p_sum[:, :], prob[s % 2][:, :], ALU.add).then_inc(p_summed, 1)
                        if chain and s == 2:
                            norm_scale(2, c)
                        if prepare and s == 4:
                            norm_scale(0, b)
                    if chain:
                        norm_scale(3, c)
                    if attend:
                        norm_scale(1, a)

                iterations(pool, body)

            @block.scalar
            def _(act):
                def normalize(i, b, to, src):
                    act.wait_ge(shift_ready[i], nth(1, b, 1))
                    nc.scalar.activation(to[:, :], src[:, :], ACT.Identity, bias=shift[i][:, :],
                                         scale=rstd[i][:, :]).then_inc(normed[i], 1)

                def transposed_half(i, c):
                    act.wait_ge(xnT_done[i], nth(2, c, 1))
                    nc.scalar.activation(tile4(xnT, 0), shared[0][:, :], ACT.Identity).then_inc(xnT_a_ready[i], 1)

                def body(k, prepare, attend, chain):
                    b, a, c = k, k - 1, k - 2
                    if chain:
                        act.wait_ge(xnT_done[3], nth(2, c - 1, 2))
                        normalize(1, c, xn_c, x1)
                        act.wait_ge(low_done, nth(1, c - 1, 1))
                        transposed_half(1, c)
                    if chain:
                        act.wait_ge(r_max_ready, nth(1, c, 1))
                        nc.scalar.activation(r_exp[0][:, :], shared[0][:, 0:E], ACT.Exp, bias=r_max[0][:, :],
                                             accum_out=r_sum[0][:, :]).then_inc(r_exp_ready, 1)
                        act.wait_ge(routeT_done, nth(1, c, 1))
                        act.wait_ge(oscale_done, nth(2, c - 1, 2))
                        nc.scalar.activation(route3T[:, :], shared[1][0:96, 0:P], ACT.Identity).then_inc(routeT_ready, 1)
                    if attend:
                        act.wait_ge(kw_done, nth(2, a, 1))
                        act.wait_ge(kwT_done, nth(2, a - 1, 2))
                        nc.scalar.activation(kw[:, half(0)], acc[:, half(0)], ACT.Identity).then_inc(kw_ready, 1)
                    if chain:
                        for h in range(2):
                            act.wait_ge(y_ready, nth(2, c, h + 1))
                            act.wait_ge(ffn_done, nth(2, c - 1, 2))
                            nc.scalar.activation(tile4(y_hi, h), tile4(xnT, h), ACT.Identity).then_inc(y_hi_ready, 1)
                    if chain:
                        for h in range(2):
                            act.wait_ge(oscale_done, nth(2, c, h + 1))
                            act.wait_ge(x2_ready, nth(2, c - 1, 2))
                            nc.scalar.activation(oscale[:, half(h)], shared[h][:, :], ACT.Identity).then_inc(oscale_ready, 1)
                    if attend:
                        act.wait_ge(kw_done, nth(2, a, 2))
                        nc.scalar.activation(kw[:, half(1)], acc[:, half(1)], ACT.Identity).then_inc(kw_ready, 1)
                    if attend:
                        for h in range(2):
                            act.wait_ge(max_turned, nth(2, a, h + 1))
                            nc.scalar.activation(q_hm[DQK:DQK + 1, half(h)], scores[0][DQK:DQK + 1, half(h)],
                                                 ACT.Identity).then_inc(max_ready, 1)
                    for s in range(T):
                        if attend:
                            act.wait_ge(scores_done, nth(8, a, s + 1))
                            act.wait_ge(p_lo_ready, nth(8, a, s - 1))
                            act.wait_ge(p_summed, nth(7, a, (-1, 0, 1)[s] if s < 3 else s - 2))
                            nc.scalar.activation(prob[s % 2][:, :], scores[s % 2][:, :], ACT.Exp).then_inc(exp_ready, 1)
                        if chain and s == 4:
                            act.wait_ge(y_lo_ready, nth(2, c, 2))
                            transposed_half(2, c)
                        if attend:
                            act.wait_ge(exp_ready, nth(8, a, s + 1))
                            act.wait_ge(pv_done, nth(8, a, s - 1))
                            nc.scalar.activation(p_hi[s % 2][:, :], prob[s % 2][:, :], ACT.Identity).then_inc(p_hi_ready, 1)
                        if chain and s == 3:
                            act.wait_ge(xnT_done[1], nth(2, c, 2))
                            normalize(2, c, xn_c, res)
                        if chain and s == 6:
                            act_chain.begin(c)
                            act.wait_ge(s_max_ready, nth(1, c, 1))
                            act_chain.chain(act, nc.scalar.activation(r_bias[:, :], r_max[1][:, :], ACT.Identity, scale=SCALE1))
                            act_chain.end()
                            act.wait_ge(attnT_done, nth(1, c - 1, 1))
                            nc.scalar.activation(attn[:, :], shared[0][:, 0:P], ACT.Exp, bias=r_bias[:, :], scale=SCALE1,
                                                 accum_out=r_sum[1][:, :]).then_inc(attn_ready, 1)
                        if prepare and s == 6:
                            normalize(0, b, xn, xn)
                        if chain and s == 6:
                            act.wait_ge(attnT_done, nth(1, c, 1))
                            act.wait_ge(att_done, nth(2, c - 1, 2))
                            nc.scalar.activation(attnT[:, :], shared[1][:, 0:P], ACT.Identity).then_inc(attnT_ready, 1)
                    if prepare:
                        for h in range(2):
                            act.wait_ge(q_done, nth(2, b, h + 1))
                            nc.scalar.activation(q_hl[:, half(h)], scores[0][:, half(h)], ACT.Identity, bias=bq_col[:, :])
                            nc.scalar.activation(q_hm[0:DQK, half(h)], scores[0][0:DQK, half(h)], ACT.Identity,
                                                 bias=bq_col[0:DQK, :]).then_inc(q_hi_ready, 1)
                    if attend:
                        for h in range(2):
                            act.wait_ge(den_turned, nth(2, a, h + 1))
                            act.wait_ge(x1_ready, nth(2, a - 1, 2))
                            nc.scalar.activation(den_rows[:, half(h)], scores[1][:, half(h)], ACT.Identity).then_inc(den_rows_ready, 1)
                    if prepare:
                        act.wait_ge(cT_done, nth(2, b, 1))
                        act.wait_ge(kw_done, nth(2, b - 1, 2))
                        nc.scalar.activation(tile4(cT, 0), shared[0][:, :], ACT.Identity).then_inc(cT_a_ready, 1)
                    if chain:
                        act.wait_ge(xnT_done[2], nth(2, c, 2))
                        normalize(3, c, xn_c, res)
                    if prepare:
                        for h in range(2):
                            act.wait_ge(k_done, nth(2, b, h + 1))
                            nc.scalar.activation(k_hh[:, half(h)], scores[1][:, half(h)], ACT.Identity,
                                                 bias=bk_col[:, :]).then_inc(k_hi_ready, 1)
                        act.wait_ge(v_done, nth(2, b, 1))
                        act.wait_ge(pv_done, nth(8, b - 1, 8))
                        nc.scalar.activation(tile4(v_hi, 0), scores[0][:, half(0)], ACT.Identity).then_inc(v_hi_ready, 1)
                    if chain:
                        act.wait_ge(sc1_done, nth(1, c, 1))
                        transposed_half(3, c)
                    if prepare:
                        act.wait_ge(v_done, nth(2, b, 2))
                        nc.scalar.activation(tile4(v_hi, 1), scores[0][:, half(1)], ACT.Identity).then_inc(v_hi_ready, 1)
                    if chain:
                        act.wait_ge(l_max_ready, nth(1, c, 1))
                        nc.scalar.activation(r_exp[1][:, :], logit[:, :], ACT.Exp, bias=r_max[2][:, :],
                                             accum_out=r_sum[2][:, :]).then_inc(l_exp_ready, 1)
                        act.wait_ge(lowT_done, nth(1, c, 1))
                        act.wait_ge(out_done, nth(2, c - 1, 2))
                        nc.scalar.activation(low_T[:, :], shared[1][:, 0:P], ACT.Identity).then_inc(lowT_ready, 1)

                iterations(act, body)

            @block.vector
            def _(dve):
                nc.vector.memset(k_l1[DQK:DQK + 1, :].bitcast(F32), 1.0).then_inc(const_made, 1)
                nc.vector.memset(neg_max[:, :], 0.0).then_inc(const_made, 1)
                nc.vector.memset(route3[:, :].bitcast(F32), 0.0).then_inc(const_made, 1)
                dve.wait_ge(const_made, 3)

                def statistics(steps, i, b, src):
                    dve.wait_ge(shift_ready[i], nth(1, b - 1, 1))
                    nc.vector.bn_stats(stat[i][:, 0:6], src[:, half(0)])
                    steps.chain(dve, nc.vector.bn_stats(stat[i][:, 6:12], src[:, half(1)]))
                    nc.vector.memset(var_eps[i][:, :], EPS)
                    steps.chain(dve, nc.vector.bn_aggr(mean_var[i][:, :], stat[i][:, :]))
                    nc.vector.tensor_scalar(neg_mean[i][:, :], mean_var[i][:, 0:1], -1.0, None, ALU.mult)
                    nc.vector.tensor_tensor(var_eps[i][:, :], mean_var[i][:, 1:2], var_eps[i][:, :], ALU.add).then_inc(var_ready[i], 1)

                def row_maximum(a, t):
                    dve.wait_ge(maxscores_done, nth(8, a, t + 1))
                    dve.wait_ge(max_turned, nth(2, a - 1, 2))
                    nc.vector.tensor_reduce(neg_max[:, DQK + t:DQK + t + 1], scores[(t + 1) % 2][:, :], AX_X, ALU.max,
                                            negate=True).then_inc(row_max, 1)

                def transposed_half(i, c):
                    dve.wait_ge(xnT_done[i], nth(2, c, 2))
                    nc.vector.tensor_copy(tile4(xnT, 1), shared[1][:, :]).then_inc(xnT_b_ready[i], 1)

                def keys_turned(a, h):
                    dve.wait_ge(sc1_done, nth(1, a - 1, 1))
                    dve.wait_ge(kwT_done, nth(2, a, 2 - h))
                    nc.vector.tensor_tensor(kwT[:, 4 * h:4 * h + 4, :], shared[h][:, :].rearrange("p (t c) -> p t c", t=4),
                                            key_bias[:, 4 * h:4 * h + 4].unsqueeze(2).to_broadcast([P, 4, P]),
                                            ALU.add).then_inc(kwT_ready, 1)

                def half_of_x2(c, h):
                    dve.wait_ge(ffn_done, nth(2, c, h + 1))
                    dve.wait_ge(oscale_ready, nth(2, c, h + 1))
                    dve_chain.chain(dve, nc.vector.tensor_tensor(oscale[:, half(h)], shared[h][:, :], oscale[:, half(h)], ALU.mult))
                    nc.vector.tensor_tensor(res[:, half(h)], res[:, half(h)], oscale[:, half(h)], ALU.add).then_inc(x2_ready, 1)

                def body(k, prepare, attend, chain):
                    b, a, c = k, k - 1, k - 2
                    if chain:
                        dve_chain.begin(c)
                    if attend:
                        dve_attend.begin(a)
                        row_maximum(a, 0)
                    if chain:
                        dve.wait_ge(low_done, nth(1, c - 1, 1))
                        transposed_half(1, c)
                    if attend:
                        row_maximum(a, 1)
                        row_maximum(a, 2)
                    if chain:
                        dve.wait_ge(route_done, nth(1, c, 1))
                        nc.vector.tensor_reduce(r_max[0][:, :], shared[0][:, 0:E], AX_X, ALU.max,
                                                negate=True).then_inc(r_max_ready, 1)
                    if attend:
                        row_maximum(a, 3)
                    if chain:
                        dve.wait_ge(r_exp_ready, nth(1, c, 1))
                        dve_chain.chain(dve, nc.vector.reciprocal(r_inv[0][:, :], r_sum[0][:, :]))
                        dve_chain.chain(dve, nc.vector.tensor_scalar(route[:, :], r_exp[0][:, :], r_inv[0][:, :], None, ALU.mult))
                        dve.wait_ge(routeT_done, nth(1, c - 1, 1))
                        nc.vector.tensor_copy(route3[:, 0:E], route[:, :])
                        dve_chain.chain(dve, nc.vector.tensor_copy(route3[:, 64:64 + E], route[:, :]))
                        nc.vector.tensor_tensor(route3[:, 32:32 + E], route[:, :], route3[:, 0:E].bitcast(F32),
                                                ALU.subtract).then_inc(route_ready, 1)
                    if attend:
                        row_maximum(a, 4)
                        row_maximum(a, 5)
                    if chain:
                        for h in range(2):
                            dve.wait_ge(iscale_done, nth(2, c, h + 1))
                            nc.vector.tensor_tensor(tile4(xnT, h), tile4(xnT, h), shared[h][:, :], ALU.mult).then_inc(y_ready, 1)
                    if attend:
                        row_maximum(a, 6)
                    if chain:
                        for h in range(2):
                            dve.wait_ge(y_hi_ready, nth(2, c, h + 1))
                            dve.wait_ge(ffn_done, nth(2, c - 1, 2))
                            nc.vector.tensor_tensor(tile4(y_lo, h), tile4(xnT, h), tile4(y_hi, h).bitcast(F32),
                                                    ALU.subtract).then_inc(y_lo_ready, 1)
                    if attend:
                        row_maximum(a, 7)
                    if chain:
                        dve.wait_ge(val_loaded, nth(16, c, 16))
                        dve.wait_ge(sc1_done, nth(1, c - 1, 1))
                        dve_chain.chain(dve, nc.vector.tensor_tensor_reduce(
                            out=den_rows[:, :], in0=c_val[:, :], in1=query_bias[:, :], scale=1.0, scalar=0.0,
                            op0=ALU.mult, op1=ALU.add, accum_out=key_sum[:, :]))
                        nc.vector.tensor_tensor(key_col[:, :], key_sum[:, :], bqbk[:, :], ALU.add).then_inc(key_col_ready, 1)
                        dve.wait_ge(biased, nth(1, c, 1))
                    for s in range(T):
                        if attend:
                            dve.wait_ge(p_hi_ready, nth(8, a, s + 1))
                            dve.wait_ge(pv_done, nth(8, a, s - 1))
                            nc.vector.tensor_tensor(p_lo[s % 2][:, :], prob[s % 2][:, :], p_hi[s % 2][:, :].bitcast(F32),
                                                    ALU.subtract).then_inc(p_lo_ready, 1)
                        if chain and s == 1:
                            half_of_x2(c, 0)
                            half_of_x2(c, 1)
                            dve.wait_ge(x2_ready, nth(2, c, 2))
                            statistics(dve_chain, 2, c, res)
                        if chain and s == 3:
                            transposed_half(2, c)
                        if prepare and s == 2:
                            dve.wait_ge(xn_loaded, nth(16, b, 16))
                            dve_prepare.begin(b)
                            statistics(dve_prepare, 0, b, xn)
                            dve_prepare.end()
                        if chain and s == 4:
                            dve.wait_ge(sc1_done, nth(1, c, 1))
                            nc.vector.tensor_reduce(r_max[1][:, :], shared[0][:, 0:P], AX_X, ALU.max,
                                                    negate=True).then_inc(s_max_ready, 1)
                        if attend and s in (4, 6):
                            keys_turned(a, (6 - s) // 2)
                        if chain and s == 6:
                            dve.wait_ge(attn_ready, nth(1, c, 1))
                            dve_chain.chain(dve, nc.vector.reciprocal(r_inv[1][:, :], r_sum[1][:, :]))
                    if chain:
                        for h in range(2):
                            dve.wait_ge(att_done, nth(2, c, h + 1))
                            nc.vector.scalar_tensor_tensor(res[:, half(h)], shared[h][:, :], r_inv[1][:, :], res[:, half(h)],
                                                           ALU.mult, ALU.add).then_inc(x3_ready, 1)
                    if attend:
                        dve.wait_ge(den_done, nth(1, a, 1))
                        dve.wait_ge(den_turned, nth(2, a - 1, 2))
                        nc.vector.reciprocal(den_inv[:, :], scores[1][:, 0:T * T].rearrange("p (t e) -> p t e", t=T)[:, :, 0]
                                             ).then_inc(den_inv_ready, 1)
                    if chain:
                        dve.wait_ge(x3_ready, nth(2, c, 2))
                        statistics(dve_chain, 3, c, res)
                    if prepare:
                        for h in range(2):
                            dve.wait_ge(q_hi_ready, nth(2, b, h + 1))
                            nc.vector.scalar_tensor_tensor(q_hl[DQK:P, half(h)], scores[0][DQK:P, half(h)], bq_col[DQK:P, :],
                                                           q_hl[DQK:P, half(h)].bitcast(F32), ALU.add,
                                                           ALU.subtract).then_inc(q_ready, 1)
                        dve.wait_ge(cT_done, nth(2, b, 2))
                        dve.wait_ge(kw_done, nth(2, b - 1, 2))
                        nc.vector.tensor_copy(tile4(cT, 1), shared[1][:, :]).then_inc(cT_b_ready, 1)
                    if attend:
                        dve.wait_ge(pv_done, nth(8, a, 8))
                        dve.wait_ge(x1_loaded, nth(16, a, 16))
                        for h in range(2):
                            dve.wait_ge(den_rows_ready, nth(2, a, h + 1))
                            dve_attend.chain(dve, nc.vector.tensor_tensor(den_rows[:, half(h)], acc[:, half(h)], den_rows[:, half(h)], ALU.mult))
                            nc.vector.scalar_tensor_tensor(x1[:, half(h)], den_rows[:, half(h)], bv_col[:, :], x1[:, half(h)],
                                                           ALU.add, ALU.add).then_inc(x1_ready, 1)
                    if chain:
                        transposed_half(3, c)
                    if attend:
                        dve.wait_ge(x1_ready, nth(2, a, 2))
                        statistics(dve_attend, 1, a, x1)
                        dve_attend.end()
                    if chain:
                        dve.wait_ge(low_done, nth(1, c, 1))
                        dve_chain.chain(dve, nc.vector.tensor_tensor(logit[:, :], shared[0][:, HR:HR + E], br_rows[:, :], ALU.add))
                        nc.vector.tensor_reduce(r_max[2][:, :], logit[:, :], AX_X, ALU.max, negate=True).then_inc(l_max_ready, 1)
                        dve.wait_ge(l_exp_ready, nth(1, c, 1))
                        dve_chain.chain(dve, nc.vector.reciprocal(r_inv[2][:, :], r_sum[2][:, :]))
                        dve_chain.chain(dve, nc.vector.tensor_scalar(route1[:, :], r_exp[1][:, :], r_inv[2][:, :], LORA, ALU.mult, ALU.mult))
                        dve.wait_ge(lowT_done, nth(1, c - 1, 1))
                        nc.vector.tensor_tensor(low[:, :].rearrange("p (h r) -> p h r", h=E),
                                                shared[0][:, 0:HR].rearrange("p (h r) -> p h r", h=E),
                                                route1[:, :].unsqueeze(2).to_broadcast([P, E, R]), ALU.mult).then_inc(low_ready, 1)
                    if prepare:
                        for h in range(2):
                            dve.wait_ge(k_hi_ready, nth(2, b, h + 1))
                            nc.vector.scalar_tensor_tensor(k_l1[0:DQK, half(h)], scores[1][0:DQK, half(h)], bk_col[0:DQK, :],
                                                           k_hh[0:DQK, half(h)].bitcast(F32), ALU.add,
                                                           ALU.subtract).then_inc(k_ready, 1)
                    if prepare:
                        for h in range(2):
                            dve.wait_ge(v_hi_ready, nth(2, b, h + 1))
                            nc.vector.tensor_tensor(tile4(v_lo, h), scores[0][:, half(h)], tile4(v_hi, h).bitcast(F32),
                                                    ALU.subtract).then_inc(v_ready, 1)
                    if chain:
                        dve.wait_ge(stored, nth(16, c - 1, 16))
                        for h in range(2):
                            dve.wait_ge(out_done, nth(2, c, h + 1))
                            nc.vector.tensor_tensor(result[:, half(h)], shared[h][:, :], res[:, half(h)], ALU.add).then_inc(out_ready, 1)
                        dve_chain.end()

                iterations(dve, body)

            @block.tensor
            def _(pe):
                mm = nc.tensor.matmul
                pe.wait_ge(const_made, 3)

                def transposes(h, src, semaphore):
                    for j in range(4):
                        t = 4 * h + j
                        last = nc.tensor.transpose(shared[h][:, j * P:(j + 1) * P], src[:, t * P:(t + 1) * P], ident[:, :])
                    last.then_inc(semaphore, 1)

                def values(h):
                    for t in range(4 * h, 4 * h + 4):
                        last = mm(scores[0][:, t * P:(t + 1) * P], xn[:, t * P:(t + 1) * P], wvT[:, :], start=True, stop=True)
                    last.then_inc(v_done, 1)

                def query_scores(a, t):
                    if t == 0:
                        pe.wait_ge(q_ready, nth(2, a, 2))
                        pe.wait_ge(k_ready, nth(2, a, 2))
                    elif t == 1:
                        pe.wait_ge(v_ready, nth(2, a, 2))
                    else:
                        pe.wait_ge(row_max, nth(8, a, t - 1))
                    for h in range(2):
                        last = mm(scores[(t + 1) % 2][:, half(h)], q_hl[:, t * P:(t + 1) * P], k_hh[:, half(h)], start=True, stop=True)
                    last.then_inc(maxscores_done, 1)

                def keys_through_queries(a, units):
                    for u in units:
                        h, f = u // T, u % T
                        if u == 0:
                            pe.wait_ge(x1_ready, nth(2, a - 1, 2))
                            pe.wait_ge(cT_a_ready, nth(1, a, 1))
                            pe.wait_ge(cT_b_ready, nth(1, a, 1))
                        last = mm(acc[:, half(h)], cT[:, f, :], mT[:, f, half(h)], start=f == 0, stop=f == T - 1)
                        if f == T - 1:
                            last.then_inc(kw_done, 1)

                def out_scale(c, h):
                    pe.wait_ge(y_ready, nth(2, c, h + 1))
                    mm(shared[h][:, :], route3T[:, :], ocs3[:, half(h)], start=True, stop=True).then_inc(oscale_done, 1)

                def feed_forward(h, fs):
                    for f in fs:
                        mm(shared[h][:, :], y_hi[:, f, :], signT[:, f, half(h)], start=f == 0, stop=False)
                        last = mm(shared[h][:, :], y_lo[:, f, :], signT[:, f, half(h)], start=False, stop=f == T - 1)
                    if f == T - 1:
                        last.then_inc(ffn_done, 1)

                def key_scores(a, s):
                    if s == 0:
                        pe.wait_ge(max_ready, nth(2, a, 2))
                    elif s == 1:
                        pe.wait_ge(row_max, nth(8, a, 7))
                    else:
                        pe.wait_ge(exp_ready, nth(8, a, s - 1))
                    for h in range(2):
                        mm(scores[s % 2][:, half(h)], k_hh[:, s * P:(s + 1) * P], q_hl[:, half(h)], start=True, stop=False)
                        last = mm(scores[s % 2][:, half(h)], k_l1[:, s * P:(s + 1) * P], q_hm[:, half(h)], start=False, stop=True)
                    last.then_inc(scores_done, 1)

                def weigh_values(a, s):
                    if s == 0:
                        pe.wait_ge(kw_ready, nth(2, a, 2))
                        pe.wait_ge(v_ready, nth(2, a, 2))
                    pe.wait_ge(p_hi_ready, nth(8, a, s + 1))
                    pe.wait_ge(p_lo_ready, nth(8, a, s + 1))
                    for v, p, first, end in ((v_hi, p_hi, s == 0, False), (v_lo, p_hi, False, False), (v_hi, p_lo, False, s == T - 1)):
                        for h in range(2):
                            last = mm(acc[:, half(h)], v[:, s, :], p[s % 2][:, half(h)], start=first, stop=end)
                    last.then_inc(pv_done, 1)

                def body(k, prepare, attend, chain):
                    b, a, c = k, k - 1, k - 2
                    for t in range(T):
                        if attend:
                            query_scores(a, t)
                        if chain and t == 1:
                            pe.wait_ge(normed[1], nth(1, c, 1))
                            for h in range(2):
                                pe.wait_ge(out_ready, nth(2, c - 1, h + 1))
                                transposes(h, xn_c, xnT_done[1])
                        if chain and t == 2:
                            pe.wait_ge(xnT_a_ready[1], nth(1, c, 1))
                            pe.wait_ge(xnT_b_ready[1], nth(1, c, 1))
                            for f in range(T):
                                last = mm(shared[0][:, 0:E], xnT[:, f, :], gateT[:, f, 0:E], start=f == 0, stop=f == T - 1)
                            last.then_inc(route_done, 1)
                        if chain and t == 4:
                            pe.wait_ge(route_ready, nth(1, c, 1))
                            nc.tensor.transpose(shared[1][0:96, 0:P], route3[:, :].bitcast(F32), ident[:, :]).then_inc(routeT_done, 1)
                        if chain and t == 5:
                            pe.wait_ge(routeT_ready, nth(1, c, 1))
                            pe.wait_ge(r_exp_ready, nth(1, c, 1))
                            for h in range(2):
                                for j in range(4):
                                    f = 4 * h + j
                                    last = mm(shared[h][:, j * P:(j + 1) * P], ics3[:, f * P:(f + 1) * P], route3T[:, :],
                                              start=True, stop=True)
                                last.then_inc(iscale_done, 1)
                        if chain and t == 6:
                            out_scale(c, 0)
                        if attend:
                            keys_through_queries(a, range(KW_UNITS[t], KW_UNITS[t + 1]))
                        if chain and t == 6:
                            out_scale(c, 1)
                    if attend:
                        pe.wait_ge(row_max, nth(8, a, 8))
                        for h in range(2):
                            for j in range(4):
                                t = 4 * h + j
                                last = nc.tensor.transpose(scores[0][0:DQK + 1, t * P:(t + 1) * P], neg_max[:, t:t + DQK + 1],
                                                           ident[:, :])
                            last.then_inc(max_turned, 1)
                    if chain:
                        pe.wait_ge(y_lo_ready, nth(2, c, 2))
                        pe.wait_ge(y_hi_ready, nth(2, c, 2))
                        pe.wait_ge(oscale_ready, nth(2, c, 1))
                        feed_forward(0, range(0, 3))
                    if attend:
                        key_scores(a, 0)
                        key_scores(a, 1)
                    if chain:
                        feed_forward(0, range(3, T))
                        pe.wait_ge(oscale_ready, nth(2, c, 2))
                        feed_forward(1, range(T))
                    for s in range(T):
                        if attend and s + 2 < T:
                            key_scores(a, s + 2)
                        if chain and s == 3:
                            pe.wait_ge(normed[2], nth(1, c, 1))
                            for h in range(2):
                                transposes(h, xn_c, xnT_done[2])
                        if chain and s == 4:
                            pe.wait_ge(xnT_a_ready[2], nth(1, c, 1))
                            pe.wait_ge(xnT_b_ready[2], nth(1, c, 1))
                            pe.wait_ge(kwT_ready, nth(2, c, 2))
                            pe.wait_ge(key_col_ready, nth(1, c, 1))
                            for f in range(T):
                                mm(shared[0][:, 0:P], xnT[:, f, :], kwT[:, f, :], start=f == 0, stop=False)
                            mm(shared[0][:, 0:P], key_col[:, :].to_broadcast([P, P]), ident[:, :], start=False,
                               stop=True).then_inc(sc1_done, 1)
                        if attend and s == 4:
                            transposes(1, kw, kwT_done)
                        if chain and s == 6:
                            pe.wait_ge(attn_ready, nth(1, c, 1))
                            pe.wait_ge(kwT_ready, nth(2, a, 1))
                            nc.tensor.transpose(shared[1][:, 0:P], attn[:, :], ident[:, :]).then_inc(attnT_done, 1)
                        if attend and s == 6:
                            transposes(0, kw, kwT_done)
                        if prepare and s == 7:
                            pe.wait_ge(c_loaded, nth(16, b, 16))
                            pe.wait_ge(exp_ready, nth(8, a, 7))
                            for h in range(2):
                                mm(scores[0][:, half(h)], wqT[:, :], c_in[:, half(h)], start=True, stop=True).then_inc(q_done, 1)
                        if chain and s == 7:
                            pe.wait_ge(attnT_ready, nth(1, c, 1))
                            pe.wait_ge(kwT_ready, nth(2, a, 2))
                            pe.wait_ge(val_loaded, nth(16, c, 16))
                            for h in range(2):
                                mm(shared[h][:, :], attnT[:, :], c_val[:, half(h)], start=True, stop=True).then_inc(att_done, 1)
                        if attend and s == 7:
                            pe.wait_ge(p_summed, nth(7, a, 7))
                            pe.wait_ge(exp_ready, nth(8, a, 8))
                            for t in range(T):
                                last = mm(scores[1][:, t * T:(t + 1) * T], p_sum[:, t * P:(t + 1) * P], ones[:, :], start=True, stop=True)
                            last.then_inc(den_done, 1)
                        if attend:
                            weigh_values(a, s)
                    if attend:
                        pe.wait_ge(den_inv_ready, nth(1, a, 1))
                        for h in range(2):
                            for j in range(4):
                                t = 4 * h + j
                                last = nc.tensor.transpose(scores[1][:, t * P:(t + 1) * P],
                                                           den_inv[:, t:t + 1].to_broadcast([P, P]), ident[:, :])
                            last.then_inc(den_turned, 1)
                    if prepare:
                        for h in range(2):
                            pe.wait_ge(x3_ready, nth(2, c, h + 1))
                            transposes(h, c_in, cT_done)
                        pe.wait_ge(den_rows_ready, nth(2, a, 2))
                        for h in range(2):
                            mm(scores[1][:, half(h)], wkT[:, :], c_in[:, half(h)], start=True, stop=True).then_inc(k_done, 1)
                        pe.wait_ge(normed[0], nth(1, b, 1))
                        pe.wait_ge(q_ready, nth(2, b, 2))
                        values(0)
                    if chain:
                        pe.wait_ge(normed[3], nth(1, c, 1))
                        for h in range(2):
                            pe.wait_ge((cT_a_ready, cT_b_ready)[h], nth(1, b, 1))
                            transposes(h, xn_c, xnT_done[3])
                    if prepare:
                        values(1)
                    if chain:
                        pe.wait_ge(xnT_a_ready[3], nth(1, c, 1))
                        pe.wait_ge(xnT_b_ready[3], nth(1, c, 1))
                        for f in range(T):
                            last = mm(shared[0][:, 0:HR + E], xnT[:, f, :], lowT[:, f, :], start=f == 0, stop=f == T - 1)
                        last.then_inc(low_done, 1)
                    if prepare:
                        keys_through_queries(b, range(0, 2))
                    if chain:
                        pe.wait_ge(low_ready, nth(1, c, 1))
                        nc.tensor.transpose(shared[1][:, 0:P], low[:, :], ident[:, :]).then_inc(lowT_done, 1)
                    if prepare:
                        keys_through_queries(b, range(2, KW_UNITS[0]))
                    if chain:
                        pe.wait_ge(lowT_ready, nth(1, c, 1))
                        for h in range(2):
                            mm(shared[h][:, :], low_T[:, :], bT[:, half(h)], start=True, stop=True).then_inc(out_done, 1)

                iterations(pe, body)


_INS = ['x', 'ctx_4096', 'L0_xattn_Wq', 'L0_xattn_bq', 'L0_xattn_Wk', 'L0_xattn_bk', 'L0_xattn_Wv', 'L0_xattn_bv',
        'L0_ffn_weight', 'L0_ffn_bias', 'L0_ffn_gate_w', 'L0_ffn_in_channel_scale', 'L0_ffn_out_channel_scale',
        'L1_xattn_Wq', 'L1_xattn_bq', 'L1_xattn_Wk', 'L1_xattn_bk', 'L1_ffn_A', 'L1_ffn_B', 'L1_ffn_Wr', 'L1_ffn_br']


def kernel(**inputs):
    import numpy as np
    import concourse.bacc as bacc
    from concourse import mybir
    from concourse.bass_utils import run_bass_kernel_spmd

    nc = bacc.Bacc("TRN2", target_bir_lowering=False, num_devices=1)
    arrays, args = {}, []
    for name in _INS:
        a = np.ascontiguousarray(inputs[name])
        arrays[f"in_{name}"] = a
        args.append(nc.dram_tensor(f"in_{name}", a.shape, mybir.dt.from_np(a.dtype), kind="ExternalInput").ap())
    args.append(nc.dram_tensor("out_x", inputs["x"].shape, mybir.dt.float32, kind="ExternalOutput").ap())
    build(nc, *args)
    return run_bass_kernel_spmd(nc, [arrays], core_ids=[0]).results[0]["out_x"]
```

```python
from contextlib import ExitStack

import concourse.bass as bass
from concourse import mybir

F32 = mybir.dt.float32
F32R = mybir.dt.float32r
ALU = mybir.AluOpType
ACT = mybir.ActivationFunctionType
AX_X = mybir.AxisListType.X

P = 128
HALF = 512
EPS = 1e-5


class Steps:

    def __init__(self, sem, per):
        self.sem, self.per = sem, per

    def begin(self, b):
        self.base, self.n = b * self.per, 0

    def chain(self, engine, instruction):
        self.n += 1
        instruction.then_inc(self.sem, 1)
        engine.wait_ge(self.sem, self.base + self.n)

    def end(self):
        assert self.n == self.per, (self.n, self.per)


def build(nc, x, ctx_, wq0, bq0, wk0, bk0, wv0, bv0, w_ffn, b_ffn, gate, ics, ocs,
          wq1, bq1, wk1, bk1, a1, b1, wr1, br1, out):
    NB, S, D = x.shape
    DQK = wq0.shape[0]
    E = gate.shape[0]
    R = a1.shape[1]
    HR = E * R
    T = D // P
    SCALE1 = float(D) ** -0.5
    LORA = 2.0 * E
    TS = T // 2
    assert S == P and HR == P and 2 * DQK == P and D == 2 * HALF

    top = ExitStack()
    with top:
        def sb(name, shape, dt=F32, stack=top):
            return stack.enter_context(nc.sbuf_tensor(name, shape, dt))

        def sem(name, stack=top):
            return stack.enter_context(nc.semaphore(name))

        ident = sb("ident", [P, P])
        ones = sb("ones", [P, T])
        minus_half = sb("minus_half", [P, 1])
        wqT_hi = sb("wqT_hi", [P, P], F32R)
        wqT_lo = sb("wqT_lo", [P, P], F32R)
        wkT_hi = sb("wkT_hi", [P, P], F32R)
        wkT_lo = sb("wkT_lo", [P, P], F32R)
        wvT = sb("wvT", [P, P])
        bq_col = sb("bq_col", [P, 1])
        bk_col = sb("bk_col", [P, 1])
        bv_col = sb("bv_col", [P, 1])
        signT = sb("signT", [P, T, D], F32R)
        gateT = sb("gateT", [P, T, 2 * E])
        ics3 = sb("ics3", [96, D], F32R)
        ocs3 = sb("ocs3", [96, D], F32R)
        bias_rows = sb("bias_rows", [P, D])
        with ExitStack() as before:
            wf_first = sb("wf_first", [P, TS, D], F32, before)
        m_hi = sb("m_hi", [P, TS, D], F32R)
        m_whole = sb("m_whole", [P, T - TS, D])
        wf_last = m_whole
        with ExitStack() as before:
            wk_nat_whole = sb("wk_nat_whole", [P, T - TS, T, P], F32, before)
        with ExitStack() as before:
            wk_lo_whole = sb("wk_lo_whole", [P, T - TS, T, P], F32R, before)
        m_lo = sb("m_lo", [P, TS, D], F32R)
        key_bias = sb("key_bias", [P, T])
        query_bias = sb("query_bias", [P, D])
        bqbk = sb("bqbk", [P, 1])
        lowT = sb("lowT", [P, T, HR + E])
        bT_hi = sb("bT_hi", [P, D], F32R)
        bT_lo = sb("bT_lo", [P, D], F32R)
        br_rows = sb("br_rows", [P, E])

        with ExitStack() as tmp:
            with ExitStack() as whole:
                wq_nat = sb("wq_nat", [P, T, D], F32, whole)
                wk_nat_split = sb("wk_nat_split", [P, TS, T, P], F32, whole)
                a_nat = sb("a_nat", [P, T, P], F32, whole)
                b_nat = sb("b_nat", [P, T, P], F32, whole)
            wq_lo = sb("wq_lo", [P, T, D], F32R, tmp)
            wk_lo_split = sb("wk_lo_split", [P, TS, T, P], F32R, tmp)
            wk_hi = [sb(f"wk_hi{i}", [P, T, P], F32R, tmp) for i in range(2)]
            wq_hi = sb("wq_hi", [P, T, D], F32R, tmp)
            bq_parts = sb("bq_parts", [P, T, 2], F32R, tmp)
            bk_parts = sb("bk_parts", [P, T, 2], F32R, tmp)
            bq_first = sb("bq_first", [P, T, 2], F32R, tmp)
            bk_first = sb("bk_first", [P, T, 2], F32R, tmp)
            f_order = list(range(TS, T)) + list(range(TS))

            def of_tile(ft, of_split, of_whole):
                return of_split[:, ft, :, :] if ft < TS else of_whole[:, ft - TS, :, :]
            small = sb("small", [P, 3, P], F32, tmp)
            g_nat = bias_rows[0:2 * E, :]
            bq1_col = sb("bq1_col", [P, T], F32, tmp)
            bk1_col = sb("bk1_col", [P, T], F32, tmp)
            ics_f = query_bias[0:96, :]
            ocs_f = sb("ocs_f", [96, D], F32, tmp)
            bk_rows = ocs_f[0:2, :]
            bq_rows = query_bias[0:2, :]
            bank = [tmp.enter_context(nc.psum_tensor(f"setup{i}", [P, HALF], F32)) for i in range(8)]
            zeroed = sem("zeroed", tmp)
            ident_made = sem("ident_made", tmp)
            ones_made = sem("ones_made", tmp)
            small_in = sem("small_in", tmp)
            scales_in = sem("scales_in", tmp)
            bias_rows_in = sem("bias_rows_in", tmp)
            low_in = sem("low_in", tmp)
            bias_in = sem("bias_in", tmp)
            wf_in = [sem(f"wf_in{i}", tmp) for i in range(2)]
            wq_in = [sem(f"wq_in{i}", tmp) for i in range(4)]
            wk_in = [sem(f"wk_in{i}", tmp) for i in range(T)]
            filled = sem("filled", tmp)
            signed = sem("signed", tmp)
            copied = sem("copied", tmp)
            split = sem("split", tmp)
            bias_split = sem("bias_split", tmp)
            wq_hi_made = sem("wq_hi_made", tmp)
            wq_lo_made = sem("wq_lo_made", tmp)
            wk_hi_made = sem("wk_hi_made", tmp)
            wk_lo_made = sem("wk_lo_made", tmp)
            m_hi_made = sem("m_hi_made", tmp)
            b_hi_made = sem("b_hi_made", tmp)
            small_hi_made = sem("small_hi_made", tmp)

            groups = ([("sign", i) for i in range(T)] + [("low", 0), ("low", 1), ("b", 0), ("b", 1)]
                      + [("sign", i) for i in range(T, 2 * T)])
            for k in range(T):
                groups += [("m", 2 * k), ("m", 2 * k + 1), ("bq_rows", k)]
                if k == 1:
                    groups += [("small", 0), ("gate", 0), ("bk_rows", 0), ("bk_rows", 1), ("bk_col", 0)]
            groups += [("query_bias", 0), ("query_bias", 1)]

            with nc.Block() as block:
                @block.sync
                def _(sp):
                    for i in range(4):
                        sp.dma_start(wq_nat[:, 2 * i:2 * i + 2, :],
                                     wq1[2 * i * P:(2 * i + 2) * P, :].rearrange("(t p) x -> p t x", p=P)).then_inc(wq_in[i], 16)
                    for i in range(2):
                        sp.dma_start((wf_first, wf_last)[i][:, :, :],
                                     w_ffn[4 * i * P:(4 * i + 4) * P, :].rearrange("(t p) h -> p t h", p=P)).then_inc(wf_in[i], 16)
                    for n, ft in enumerate(f_order):
                        sp.dma_start(of_tile(ft, wk_nat_split, wk_nat_whole),
                                     wk1[:, ft * P:(ft + 1) * P].rearrange("(t p) f -> p t f", p=P)).then_inc(wk_in[n], 16)

                @block.gpsimd
                def _(pool):
                    nc.gpsimd.memset(ident[:, :], 0.0).then_inc(ident_made, 1)
                    pool.wait_ge(ident_made, 1)
                    nc.gpsimd.affine_select(out=ident[:, :], in_=ident[:, :], compare_op=ALU.not_equal, fill=1.0,
                                            base=0, pattern=[[-1, P]], channel_multiplier=1).then_inc(ident_made, 1)
                    nc.gpsimd.memset(ones[:, :], 1.0).then_inc(ones_made, 1)
                    nc.gpsimd.memset(minus_half[:, :], -0.5)

                @block.scalar
                def _(act):
                    act.dma_start(a_nat[:, :, :].rearrange("p t d -> p (t d)"),
                                  a1.rearrange("h r d -> (h r) d")).then_inc(low_in, 16)
                    for h in range(E):
                        act.dma_start(b_nat[:, :, h * R:(h + 1) * R],
                                      b1[h].rearrange("(t p) r -> p t r", p=P)).then_inc(low_in, 16)
                    act.dma_start(bq1_col[:, :], bq1.rearrange("(t p) -> p t", p=P), allow_slow_non_contiguous=True).then_inc(bias_in, 16)
                    act.dma_start(bk1_col[:, :], bk1.rearrange("(t p) -> p t", p=P), allow_slow_non_contiguous=True).then_inc(bias_in, 16)
                    n_small = 0
                    for dst, src in (
                        (small[0:DQK, 0, :], wq0), (small[DQK:P, 0, :], wq0),
                        (small[0:DQK, 1, :], wk0), (small[DQK:P, 1, :], wk0), (small[:, 2, :], wv0),
                        (bq_col[0:DQK, :], bq0.unsqueeze(1)), (bq_col[DQK:P, :], bq0.unsqueeze(1)),
                        (bk_col[0:DQK, :], bk0.unsqueeze(1)), (bk_col[DQK:P, :], bk0.unsqueeze(1)),
                        (bv_col[:, :], bv0.unsqueeze(1)),
                        (g_nat[0:E, :], gate), (g_nat[E:2 * E, :], wr1),
                        (br_rows[:, :], br1.partition_broadcast(P)),
                    ):
                        act.dma_start(dst, src).then_inc(small_in, 16)
                        n_small += 1
                    assert n_small == 13
                    act.wait_ge(zeroed, 2)
                    for k in range(3):
                        act.dma_start(ics_f[32 * k:32 * k + E, :], ics).then_inc(scales_in, 16)
                        act.dma_start(ocs_f[32 * k:32 * k + E, :], ocs).then_inc(scales_in, 16)
                    for t in range(T):
                        act.wait_ge(wq_in[t // 2], 16)
                        nc.scalar.activation(wq_hi[:, t, :], wq_nat[:, t, :], ACT.Identity).then_inc(wq_hi_made, 1)
                    for n, (kind, i) in enumerate(groups):
                        if kind != "sign":
                            continue
                        act.wait_ge(filled, n + 1)
                        nc.scalar.activation(signT[:, i % T, (i // T) * HALF:(i // T + 1) * HALF], bank[n % 8][:, :],
                                             ACT.Sign).then_inc(signed, 1)

                    act.wait_ge(filled, groups.index(("gate", 0)) + 1)
                    act.dma_start(bias_rows[:, :], b_ffn.partition_broadcast(P)).then_inc(bias_rows_in, 16)
                    act.wait_ge(bias_rows_in, 16)

                @block.vector
                def _(dve):
                    def split_keys(n):
                        nat, lo = of_tile(f_order[n], wk_nat_split, wk_nat_whole), of_tile(f_order[n], wk_lo_split, wk_lo_whole)
                        dve.wait_ge(wk_in[n], 16)
                        nc.vector.tensor_copy(wk_hi[n % 2][:, :, :], nat).then_inc(wk_hi_made, 1)
                        dve.wait_ge(wk_hi_made, n + 1)
                        nc.vector.tensor_tensor(lo, nat, wk_hi[n % 2][:, :, :].bitcast(F32), ALU.subtract).then_inc(wk_lo_made, 1)

                    nc.vector.memset(ics_f, 0.0).then_inc(zeroed, 1)
                    nc.vector.memset(ocs_f[:, :], 0.0).then_inc(zeroed, 1)
                    nc.vector.memset(bq_first[:, :, :].bitcast(F32), 0.0).then_inc(zeroed, 1)
                    nc.vector.memset(bk_first[:, :, :].bitcast(F32), 0.0).then_inc(zeroed, 1)
                    for t in range(T):
                        dve.wait_ge(wq_hi_made, t + 1)
                        nc.vector.tensor_tensor(wq_lo[:, t, :], wq_nat[:, t, :], wq_hi[:, t, :].bitcast(F32),
                                                ALU.subtract).then_inc(wq_lo_made, 1)
                    for n, (kind, i) in enumerate(groups):
                        if kind == "sign":
                            continue
                        if (kind, i) == ("m", 0):
                            dve.wait_ge(bias_in, 2 * 16)
                            dve.wait_ge(zeroed, 4)
                            for parts, first, full in ((bq_parts, bq_first, bq1_col), (bk_parts, bk_first, bk1_col)):
                                nc.vector.tensor_copy(parts[:, :, 0], full[:, :]).then_inc(bias_split, 1)
                                nc.vector.tensor_copy(first[:, :, 0], full[:, :]).then_inc(bias_split, 1)
                            dve.wait_ge(bias_split, 4)
                            for parts, full in ((bq_parts, bq1_col), (bk_parts, bk1_col)):
                                nc.vector.tensor_tensor(parts[:, :, 1], full[:, :], parts[:, :, 0].bitcast(F32),
                                                        ALU.subtract).then_inc(bias_split, 1)
                        if (kind, i) == ("bq_rows", 0):
                            dve.wait_ge(scales_in, 6 * 16)
                            nc.vector.tensor_copy(ics3[:, :], ics_f).then_inc(split, 1)
                            nc.vector.tensor_copy(ocs3[:, :], ocs_f[:, :]).then_inc(split, 1)
                            dve.wait_ge(split, 2)
                            for hi, full in ((ics3, query_bias), (ocs3, ocs_f)):
                                nc.vector.tensor_tensor(hi[64:96, :], full[64:96, :], hi[64:96, :].bitcast(F32), ALU.subtract).then_inc(split, 1)
                            dve.wait_ge(split, 4)
                        dve.wait_ge(filled, n + 1)
                        s = bank[n % 8]
                        if kind == "small":
                            for j, (hi, lo) in enumerate(((wqT_hi, wqT_lo), (wkT_hi, wkT_lo))):
                                nc.vector.tensor_copy(hi[:, :], s[:, j * P:(j + 1) * P]).then_inc(small_hi_made, 1)
                                dve.wait_ge(small_hi_made, j + 1)
                                nc.vector.tensor_tensor(lo[:, :], s[:, j * P:(j + 1) * P], hi[:, :].bitcast(F32), ALU.subtract)
                            last = nc.vector.tensor_copy(wvT[:, :], s[:, 2 * P:3 * P])
                        elif kind == "gate":
                            nc.vector.tensor_copy(gateT[:, :, :], s[:, 0:T * 2 * E].rearrange("p (t e) -> p t e", t=T))
                            last = nc.vector.tensor_copy(
                                lowT[:, :, HR:HR + E], s[:, 0:T * 2 * E].rearrange("p (t e) -> p t e", t=T)[:, :, E:2 * E])
                        elif kind == "low":
                            last = nc.vector.tensor_copy(lowT[:, 4 * i:4 * i + 4, 0:HR],
                                                         s[:, :].rearrange("p (t e) -> p t e", t=4))
                        elif kind == "b":
                            cols = slice(i * HALF, (i + 1) * HALF)
                            nc.vector.tensor_copy(bT_hi[:, cols], s[:, :]).then_inc(b_hi_made, 1)
                            dve.wait_ge(b_hi_made, i + 1)
                            last = nc.vector.tensor_tensor(bT_lo[:, cols], s[:, :], bT_hi[:, cols].bitcast(F32), ALU.subtract)
                        elif kind == "bk_rows":
                            last = nc.vector.tensor_copy(bk_rows[:, i * HALF:(i + 1) * HALF], s[0:2, :])
                        elif kind == "bk_col":
                            nc.vector.tensor_copy(key_bias[:, :], s[:, 0:T])
                            last = nc.vector.tensor_copy(bqbk[:, :], s[:, T:T + 1])
                        elif kind == "m":
                            ft, cols = f_order[i // 2], slice((i % 2) * HALF, (i % 2 + 1) * HALF)
                            if ft < TS:
                                nc.vector.tensor_copy(m_hi[:, ft, cols], s[:, :]).then_inc(m_hi_made, 1)
                                dve.wait_ge(m_hi_made, 2 * ft + i % 2 + 1)
                                last = nc.vector.tensor_tensor(m_lo[:, ft, cols], s[:, :], m_hi[:, ft, cols].bitcast(F32), ALU.subtract)
                            else:
                                last = nc.vector.tensor_copy(m_whole[:, ft - TS, cols], s[:, :])
                        elif kind == "bq_rows":
                            last = nc.vector.tensor_copy(bq_rows[:, f_order[i] * P:(f_order[i] + 1) * P], s[0:2, 0:P])
                        else:
                            last = nc.vector.tensor_copy(query_bias[:, i * HALF:(i + 1) * HALF], s[:, :])
                        last.then_inc(copied, 1)
                        if kind == "b" and i == 1:
                            split_keys(0)
                            split_keys(1)
                        if kind == "bq_rows" and i + 2 < T:
                            split_keys(i + 2)

                @block.tensor
                def _(pe):
                    mm = nc.tensor.matmul
                    pe.wait_ge(ident_made, 2)
                    for n, (kind, i) in enumerate(groups):
                        if n >= 8:
                            by_act = groups[n - 8][0] == "sign"
                            pe.wait_ge(signed if by_act else copied,
                                       sum((g[0] == "sign") == by_act for g in groups[:n - 7]))
                        s = bank[n % 8]
                        if kind == "small":
                            pe.wait_ge(small_in, 13 * 16)
                            for j in range(3):
                                last = nc.tensor.transpose(s[:, j * P:(j + 1) * P], small[:, j, :], ident[:, :])
                        elif kind == "gate":
                            for t in range(T):
                                last = nc.tensor.transpose(s[:, t * 2 * E:(t + 1) * 2 * E], g_nat[:, t * P:(t + 1) * P],
                                                           ident[0:2 * E, 0:2 * E])
                        elif kind in ("low", "b"):
                            if kind == "low" and i == 0:
                                pe.wait_ge(low_in, 16 * (1 + E))
                            for j in range(4):
                                src = a_nat if kind == "low" else b_nat
                                last = nc.tensor.transpose(s[:, j * P:(j + 1) * P], src[:, 4 * i + j, :], ident[:, :])
                        elif kind == "sign":
                            if i % T == 0:
                                pe.wait_ge(wf_in[i // T], 16)
                            for j in range(4):
                                last = nc.tensor.transpose(s[:, j * P:(j + 1) * P],
                                                           (wf_first, wf_last)[i // T][:, j, (i % T) * P:(i % T + 1) * P], ident[:, :])
                        elif kind == "bk_rows":
                            if i == 0:
                                pe.wait_ge(bias_split, 6)
                                pe.wait_ge(wq_hi_made, T)
                                pe.wait_ge(wq_lo_made, T)
                            for t in range(T):
                                mm(s[0:2, :], bk_parts[:, t, :], wq_hi[:, t, i * HALF:(i + 1) * HALF], start=t == 0, stop=False)
                                last = mm(s[0:2, :], bk_first[:, t, :], wq_lo[:, t, i * HALF:(i + 1) * HALF], start=False, stop=t == T - 1)
                        elif kind == "bk_col":
                            pe.wait_ge(ones_made, 1)
                            pe.wait_ge(copied, sum(g[0] != "sign" for g in groups[:n]))
                            for j in range(T):
                                mm(s[:, j:j + 1], bk_rows[:, j * P:(j + 1) * P], ones[0:2, 0:1], start=True, stop=True)
                            for t in range(T):
                                last = mm(s[:, T:T + 1], bq1_col[:, t:t + 1].to_broadcast([P, P]), bk1_col[:, t:t + 1],
                                          start=t == 0, stop=t == T - 1)
                        elif kind == "m":
                            k, cols = i // 2, slice((i % 2) * HALF, (i % 2 + 1) * HALF)
                            lo = of_tile(f_order[k], wk_lo_split, wk_lo_whole)
                            if i % 2 == 0:
                                pe.wait_ge(wq_hi_made, T)
                                pe.wait_ge(wq_lo_made, T)
                                pe.wait_ge(wk_hi_made, k + 1)
                                pe.wait_ge(wk_lo_made, k + 1)
                            for t in range(T):
                                mm(s[:, :], wk_hi[k % 2][:, t, :], wq_hi[:, t, cols], start=t == 0, stop=False)
                                mm(s[:, :], wk_hi[k % 2][:, t, :], wq_lo[:, t, cols], start=False, stop=False)
                                last = mm(s[:, :], lo[:, t, :], wq_hi[:, t, cols], start=False, stop=t == T - 1)
                        elif kind == "bq_rows":
                            lo = of_tile(f_order[i], wk_lo_split, wk_lo_whole)
                            pe.wait_ge(bias_split, 6)
                            for t in range(T):
                                mm(s[0:2, 0:P], bq_parts[:, t, :], wk_hi[i % 2][:, t, :], start=t == 0, stop=False)
                                last = mm(s[0:2, 0:P], bq_first[:, t, :], lo[:, t, :], start=False, stop=t == T - 1)
                        else:
                            pe.wait_ge(copied, sum(g[0] != "sign" for g in groups[:n - i]))
                            last = mm(s[:, :], ones[0:2, 0:1].to_broadcast([2, P]), bq_rows[:, i * HALF:(i + 1) * HALF],
                                      start=True, stop=True)
                        last.then_inc(filled, 1)

        with ExitStack() as shared_memory:
            c_in = sb("c_in", [P, D], F32, shared_memory)
            xn = sb("xn", [P, D], F32, shared_memory)
        y_hi = sb("y_hi", [P, T, P], F32R)
        y_lo = sb("y_lo", [P, T, P], F32R)
        v_hi = sb("v_hi", [P, T, P], F32R)
        v_lo = sb("v_lo", [P, T, P], F32R)
        q_hl = sb("q_hl", [P, D], F32R)
        q_hm = sb("q_hm", [DQK + T, D], F32R)
        k_hh = sb("k_hh", [P, D], F32R)
        k_l1 = sb("k_l1", [DQK + T, D], F32R)
        cT_hi = sb("cT_hi", [P, TS, P], F32R)
        cT_lo = sb("cT_lo", [P, TS, P], F32R)
        cT_whole = sb("cT_whole", [P, T - TS, P])
        neg_max = sb("neg_max", [P, DQK + T])
        prob = [sb(f"prob{i}", [P, D]) for i in range(2)]
        p_hi = [sb(f"p_hi{i}", [P, D], F32R) for i in range(2)]
        p_lo = [sb(f"p_lo{i}", [P, D], F32R) for i in range(2)]
        p_sum = sb("p_sum", [P, D])
        x1 = sb("x1", [P, D])
        kw = x1
        kwT = sb("kwT", [P, T, P])
        den_inv = sb("den_inv", [P, T])
        den_rows = prob[0]
        unread = prob[1]
        res = sb("res", [P, D])
        with ExitStack() as shared_memory:
            xnT = sb("xnT", [P, T, P], F32, shared_memory)
            oscale = sb("oscale", [P, D], F32, shared_memory)
        c_hi = sb("c_hi", [P, D], F32R)
        c_lo = sb("c_lo", [P, D], F32R)
        c_val = sb("c_val", [P, D])
        stat = [sb(f"stat{i}", [P, 12]) for i in range(4)]
        mean_var = [sb(f"mean_var{i}", [P, 2]) for i in range(4)]
        neg_mean = [sb(f"neg_mean{i}", [P, 1]) for i in range(4)]
        var_eps = [sb(f"var_eps{i}", [P, 1]) for i in range(4)]
        rstd = [sb(f"rstd{i}", [P, 1]) for i in range(4)]
        shift = [sb(f"shift{i}", [P, 1]) for i in range(4)]
        logit = sb("logit", [P, E])
        r_max = [sb(f"r_max{i}", [P, 1]) for i in range(3)]
        r_bias = sb("r_bias", [P, 1])
        r_exp = [sb(f"r_exp{i}", [P, E]) for i in range(2)]
        r_sum = [sb(f"r_sum{i}", [P, 1]) for i in range(3)]
        r_inv = [sb(f"r_inv{i}", [P, 1]) for i in range(3)]
        route = sb("route", [P, E])
        route1 = sb("route1", [P, E])
        route3 = sb("route3", [P, 96], F32R)
        route3T = sb("route3T", [96, P], F32R)
        key_sum = sb("key_sum", [P, 1])
        key_col = sb("key_col", [P, 1])
        xn_1 = xn_3 = p_sum
        xn_2 = oscale
        result = oscale
        attn = sb("attn", [P, P])
        attnT = sb("attnT", [P, P])
        low = sb("low", [P, HR])
        lowT_hi = sb("lowT_hi", [P, P], F32R)
        lowT_lo = sb("lowT_lo", [P, P], F32R)

        def psum(name, shape):
            return top.enter_context(nc.psum_tensor(name, shape, F32))

        scores = [psum(f"scores{i}", [P, D]) for i in range(2)]
        acc = psum("acc", [P, D])
        shared = [psum(f"shared{i}", [P, HALF]) for i in range(2)]

        const_made = sem("const_made")
        c_loaded = sem("c_loaded")
        xn_loaded = sem("xn_loaded")
        x1_loaded = sem("x1_loaded")
        val_loaded = sem("val_loaded")
        stored = sem("stored")
        var_ready = [sem(f"var_ready{i}") for i in range(4)]
        shift_ready = [sem(f"shift_ready{i}") for i in range(4)]
        normed = [sem(f"normed{i}") for i in range(4)]
        cT_done = sem("cT_done")
        q_done = sem("q_done")
        k_done = sem("k_done")
        v_done = sem("v_done")
        maxscores_done = sem("maxscores_done")
        kw_done = sem("kw_done")
        max_turned = sem("max_turned")
        scores_done = sem("scores_done")
        pv_done = sem("pv_done")
        den_done = sem("den_done")
        den_turned = sem("den_turned")
        kwT_done = sem("kwT_done")
        xnT_done = [None] + [sem(f"xnT_done{i}") for i in (1, 2, 3)]
        route_done = sem("route_done")
        routeT_done = sem("routeT_done")
        iscale_done = sem("iscale_done")
        oscale_done = sem("oscale_done")
        ffn_done = sem("ffn_done")
        sc1_done = sem("sc1_done")
        attnT_done = sem("attnT_done")
        att_done = sem("att_done")
        low_done = sem("low_done")
        lowT_done = sem("lowT_done")
        out_done = sem("out_done")
        cT_hi_ready = sem("cT_hi_ready")
        cT_lo_ready = sem("cT_lo_ready")
        cT_whole_ready = sem("cT_whole_ready")
        c_hi_ready = sem("c_hi_ready")
        c_lo_ready = sem("c_lo_ready")
        k_hi_ready = sem("k_hi_ready")
        q_hi_ready = sem("q_hi_ready")
        q_ready = sem("q_ready")
        k_ready = sem("k_ready")
        v_hi_ready = sem("v_hi_ready")
        v_ready = sem("v_ready")
        row_max = sem("row_max")
        kw_ready = sem("kw_ready")
        max_ready = sem("max_ready")
        exp_ready = sem("exp_ready")
        p_hi_ready = sem("p_hi_ready")
        p_lo_ready = sem("p_lo_ready")
        p_summed = sem("p_summed")
        den_inv_ready = sem("den_inv_ready")
        den_rows_ready = sem("den_rows_ready")
        x1_ready = sem("x1_ready")
        kwT_ready = sem("kwT_ready")
        key_col_ready = sem("key_col_ready")
        xnT_a_ready = [None] + [sem(f"xnT_a_ready{i}") for i in (1, 2, 3)]
        xnT_b_ready = [None] + [sem(f"xnT_b_ready{i}") for i in (1, 2, 3)]
        biased = sem("biased")
        r_max_ready = sem("r_max_ready")
        r_exp_ready = sem("r_exp_ready")
        route_ready = sem("route_ready")
        routeT_ready = sem("routeT_ready")
        y_ready = sem("y_ready")
        y_hi_ready = sem("y_hi_ready")
        y_lo_ready = sem("y_lo_ready")
        oscale_ready = sem("oscale_ready")
        x2_ready = sem("x2_ready")
        s_max_ready = sem("s_max_ready")
        attn_ready = sem("attn_ready")
        attnT_ready = sem("attnT_ready")
        x3_ready = sem("x3_ready")
        l_max_ready = sem("l_max_ready")
        l_exp_ready = sem("l_exp_ready")
        low_ready = sem("low_ready")
        lowT_hi_ready = sem("lowT_hi_ready")
        lowT_lo_ready = sem("lowT_lo_ready")
        out_ready = sem("out_ready")
        dve_prepare = Steps(sem("dve_prepare"), 2)
        dve_attend = Steps(sem("dve_attend"), 4)
        dve_chain = Steps(sem("dve_chain"), 14)
        pool_norm = [Steps(sem(f"pool_norm{i}"), 1) for i in range(4)]
        act_chain = Steps(sem("act_chain"), 1)

        KW_UNITS = (4, 5, 7, 8, 11, 12, 13, 14, 16)

        def half(h):
            return slice(h * HALF, (h + 1) * HALF)

        def tile4(buf, h):
            return buf[:, 4 * h:4 * h + 4, :].rearrange("p t c -> p (t c)")

        def nth(per, b, n):
            if isinstance(b, int):
                return max(0, per * min(b, NB - 1) + n)
            return b * per + n

        def iterations(engine, body):
            for k in range(3):
                body(k, True, k >= 1, k >= 2)
            with engine.Fori(3, NB) as k:
                body(k, True, True, True)
            body(NB, False, True, True)
            body(NB + 1, False, False, True)

        with nc.Block() as block:

            @block.sync
            def _(sp):
                def body(k, prepare, attend, chain):
                    b, a, c = k, k - 1, k - 2
                    if chain:
                        sp.wait_ge(att_done, nth(2, c - 1, 2))
                        sp.dma_start(c_val[:, :], ctx_[c]).then_inc(val_loaded, 16)
                    if prepare:
                        sp.wait_ge(ffn_done, nth(2, c, 2))
                        sp.wait_ge(cT_done, nth(2, b - 1, 2))
                        sp.dma_start(c_in[:, :], ctx_[b]).then_inc(c_loaded, 16)
                        sp.wait_ge(v_done, nth(2, b - 1, 2))
                        sp.dma_start(xn[:, :], x[b]).then_inc(xn_loaded, 16)
                    if attend:
                        sp.wait_ge(kwT_done, nth(2, a, 2))
                        sp.dma_start(x1[:, :], x[a]).then_inc(x1_loaded, 16)
                    if chain:
                        sp.wait_ge(out_ready, nth(2, c, 2))
                        sp.dma_start(out[c], result[:, :]).then_inc(stored, 16)

                iterations(sp, body)
                sp.wait_ge(stored, 16 * NB)

            @block.gpsimd
            def _(pool):
                def norm_scale(i, b):
                    pool.wait_ge(var_ready[i], nth(1, b, 1))
                    pool.wait_ge(normed[i], nth(1, b - 1, 1))
                    pool_norm[i].begin(b)
                    pool_norm[i].chain(pool, nc.gpsimd.tensor_tensor(rstd[i][:, :], var_eps[i][:, :], minus_half[:, :], ALU.pow))
                    nc.gpsimd.tensor_tensor(shift[i][:, :], neg_mean[i][:, :], rstd[i][:, :], ALU.mult).then_inc(shift_ready[i], 1)
                    pool_norm[i].end()

                def body(k, prepare, attend, chain):
                    b, a, c = k, k - 1, k - 2
                    if chain:
                        pool.wait_ge(x1_ready, nth(2, c, 2))
                        pool.wait_ge(out_ready, nth(2, c - 1, 2))
                        nc.gpsimd.tensor_tensor(res[:, :], x1[:, :], bias_rows[:, :], ALU.add).then_inc(biased, 1)
                    for s in range(T):
                        if attend and s >= 1:
                            pool.wait_ge(exp_ready, nth(8, a, s + 1))
                            if s == 1:
                                pool.wait_ge(xnT_done[1], nth(2, c, 2))
                                pool.wait_ge(den_done, nth(1, a - 1, 1))
                                nc.gpsimd.tensor_tensor(p_sum[:, :], prob[0][:, :], prob[1][:, :], ALU.add).then_inc(p_summed, 1)
                            else:
                                pool.wait_ge(p_summed, nth(7, a, s - 1))
                                nc.gpsimd.tensor_tensor(p_sum[:, :], p_sum[:, :], prob[s % 2][:, :], ALU.add).then_inc(p_summed, 1)
                        if chain and s == 2:
                            norm_scale(2, c)
                        if prepare and s == 4:
                            norm_scale(0, b)
                    if chain:
                        norm_scale(3, c)
                    if attend:
                        norm_scale(1, a)

                iterations(pool, body)

            @block.scalar
            def _(act):
                def normalize(i, b, to, src):
                    act.wait_ge(shift_ready[i], nth(1, b, 1))
                    nc.scalar.activation(to[:, :], src[:, :], ACT.Identity, bias=shift[i][:, :],
                                         scale=rstd[i][:, :]).then_inc(normed[i], 1)

                def transposed_half(i, c):
                    act.wait_ge(xnT_done[i], nth(2, c, 1))
                    nc.scalar.activation(tile4(xnT, 0), shared[0][:, :], ACT.Identity).then_inc(xnT_a_ready[i], 1)

                def body(k, prepare, attend, chain):
                    b, a, c = k, k - 1, k - 2
                    if chain:
                        act.wait_ge(xnT_done[3], nth(2, c - 1, 2))
                        normalize(1, c, xn_1, x1)
                        act.wait_ge(low_done, nth(1, c - 1, 1))
                        transposed_half(1, c)
                    if chain:
                        act.wait_ge(r_max_ready, nth(1, c, 1))
                        nc.scalar.activation(r_exp[0][:, :], shared[0][:, 0:E], ACT.Exp, bias=r_max[0][:, :],
                                             accum_out=r_sum[0][:, :]).then_inc(r_exp_ready, 1)
                        act.wait_ge(routeT_done, nth(1, c, 1))
                        act.wait_ge(oscale_done, nth(2, c - 1, 2))
                        nc.scalar.activation(route3T[:, :], shared[1][0:96, 0:P], ACT.Identity).then_inc(routeT_ready, 1)
                    if attend:
                        act.wait_ge(kw_done, nth(2, a, 1))
                        act.wait_ge(biased, nth(1, a - 1, 1))
                        nc.scalar.activation(kw[:, half(0)], acc[:, half(0)], ACT.Identity).then_inc(kw_ready, 1)
                    if chain:
                        for h in range(2):
                            act.wait_ge(y_ready, nth(2, c, h + 1))
                            act.wait_ge(ffn_done, nth(2, c - 1, 2))
                            nc.scalar.activation(tile4(y_hi, h), tile4(xnT, h), ACT.Identity).then_inc(y_hi_ready, 1)
                    if chain:
                        for h in range(2):
                            act.wait_ge(oscale_done, nth(2, c, h + 1))
                            act.wait_ge(stored, nth(16, c - 1, 16))
                            nc.scalar.activation(oscale[:, half(h)], shared[h][:, :], ACT.Identity).then_inc(oscale_ready, 1)
                    if attend:
                        act.wait_ge(kw_done, nth(2, a, 2))
                        nc.scalar.activation(kw[:, half(1)], acc[:, half(1)], ACT.Identity).then_inc(kw_ready, 1)
                    for s in range(T):
                        if chain and s == 1:
                            act.wait_ge(key_col_ready, nth(1, c, 1))
                        if attend:
                            act.wait_ge(scores_done, nth(8, a, s + 1))
                            act.wait_ge(p_lo_ready, nth(8, a, s - 1))
                            act.wait_ge(p_summed, nth(7, a, (-1, 0, 1)[s] if s < 3 else s - 2))
                            nc.scalar.activation(prob[s % 2][:, :], scores[s % 2][:, :], ACT.Exp).then_inc(exp_ready, 1)
                        if chain and s == 4:
                            act.wait_ge(y_lo_ready, nth(2, c, 2))
                            transposed_half(2, c)
                        if attend:
                            act.wait_ge(exp_ready, nth(8, a, s + 1))
                            act.wait_ge(pv_done, nth(8, a, s - 1))
                            nc.scalar.activation(p_hi[s % 2][:, :], prob[s % 2][:, :], ACT.Identity).then_inc(p_hi_ready, 1)
                        if chain and s == 3:
                            act.wait_ge(x2_ready, nth(2, c, 2))
                            normalize(2, c, xn_2, res)
                        if chain and s == 6:
                            act_chain.begin(c)
                            act.wait_ge(s_max_ready, nth(1, c, 1))
                            act_chain.chain(act, nc.scalar.activation(r_bias[:, :], r_max[1][:, :], ACT.Identity, scale=SCALE1))
                            act_chain.end()
                            act.wait_ge(attnT_done, nth(1, c - 1, 1))
                            nc.scalar.activation(attn[:, :], shared[0][:, 0:P], ACT.Exp, bias=r_bias[:, :], scale=SCALE1,
                                                 accum_out=r_sum[1][:, :]).then_inc(attn_ready, 1)
                        if prepare and s == 6:
                            normalize(0, b, xn, xn)
                        if chain and s == 6:
                            act.wait_ge(attnT_done, nth(1, c, 1))
                            act.wait_ge(att_done, nth(2, c - 1, 2))
                            nc.scalar.activation(attnT[:, :], shared[1][:, 0:P], ACT.Identity).then_inc(attnT_ready, 1)
                    if prepare:
                        for h in range(2):
                            act.wait_ge(q_done, nth(2, b, h + 1))
                            nc.scalar.activation(q_hl[:, half(h)], scores[0][:, half(h)], ACT.Identity, bias=bq_col[:, :])
                            nc.scalar.activation(q_hm[0:DQK, half(h)], scores[0][0:DQK, half(h)], ACT.Identity,
                                                 bias=bq_col[0:DQK, :]).then_inc(q_hi_ready, 1)
                    if attend:
                        for h in range(2):
                            act.wait_ge(den_turned, nth(2, a, h + 1))
                            act.wait_ge(x1_ready, nth(2, a - 1, 2))
                            nc.scalar.activation(den_rows[:, half(h)], scores[1][:, half(h)], ACT.Identity).then_inc(den_rows_ready, 1)
                    if prepare:
                        act.wait_ge(cT_done, nth(2, b, 1))
                        act.wait_ge(kw_done, nth(2, b - 1, 2))
                        nc.scalar.activation(cT_hi[:, :, :].rearrange("p t c -> p (t c)"), shared[0][:, :],
                                             ACT.Identity).then_inc(cT_hi_ready, 1)
                    if chain:
                        act.wait_ge(den_done, nth(1, a, 1))
                        normalize(3, c, xn_3, res)
                    if prepare:
                        act.wait_ge(cT_done, nth(2, b, 2))
                        nc.scalar.activation(cT_whole[:, :, :].rearrange("p t c -> p (t c)"), shared[1][:, :],
                                             ACT.Identity).then_inc(cT_whole_ready, 1)
                    if prepare:
                        for h in range(2):
                            act.wait_ge(k_done, nth(2, b, h + 1))
                            nc.scalar.activation(k_hh[:, half(h)], scores[1][:, half(h)], ACT.Identity,
                                                 bias=bk_col[:, :]).then_inc(k_hi_ready, 1)
                    if chain:
                        act.wait_ge(sc1_done, nth(1, c, 1))
                        transposed_half(3, c)
                    if prepare:
                        act.wait_ge(v_done, nth(2, b, 1))
                        act.wait_ge(pv_done, nth(8, b - 1, 8))
                        nc.scalar.activation(tile4(v_hi, 0), scores[0][:, half(0)], ACT.Identity).then_inc(v_hi_ready, 1)
                        act.wait_ge(v_done, nth(2, b, 2))
                        nc.scalar.activation(tile4(v_hi, 1), scores[0][:, half(1)], ACT.Identity).then_inc(v_hi_ready, 1)
                    if chain:
                        act.wait_ge(l_max_ready, nth(1, c, 1))
                        nc.scalar.activation(r_exp[1][:, :], logit[:, :], ACT.Exp, bias=r_max[2][:, :],
                                             accum_out=r_sum[2][:, :]).then_inc(l_exp_ready, 1)
                        act.wait_ge(lowT_done, nth(1, c, 1))
                        act.wait_ge(out_done, nth(2, c - 1, 2))
                        nc.scalar.activation(lowT_hi[:, :], shared[1][:, 0:P], ACT.Identity).then_inc(lowT_hi_ready, 1)

                iterations(act, body)

            @block.vector
            def _(dve):
                nc.vector.memset(k_l1[DQK:DQK + T, :].bitcast(F32), 1.0).then_inc(const_made, 1)
                nc.vector.memset(neg_max[:, :], 0.0).then_inc(const_made, 1)
                nc.vector.memset(route3[:, :].bitcast(F32), 0.0).then_inc(const_made, 1)
                dve.wait_ge(const_made, 3)

                def statistics(steps, i, b, src):
                    dve.wait_ge(shift_ready[i], nth(1, b - 1, 1))
                    nc.vector.bn_stats(stat[i][:, 0:6], src[:, half(0)])
                    steps.chain(dve, nc.vector.bn_stats(stat[i][:, 6:12], src[:, half(1)]))
                    nc.vector.memset(var_eps[i][:, :], EPS)
                    steps.chain(dve, nc.vector.bn_aggr(mean_var[i][:, :], stat[i][:, :]))
                    nc.vector.tensor_scalar(neg_mean[i][:, :], mean_var[i][:, 0:1], -1.0, None, ALU.mult)
                    nc.vector.tensor_tensor(var_eps[i][:, :], mean_var[i][:, 1:2], var_eps[i][:, :], ALU.add).then_inc(var_ready[i], 1)

                def row_maximum(a, t):
                    dve.wait_ge(maxscores_done, nth(8, a, t + 1))
                    dve.wait_ge(max_turned, nth(1, a - 1, 1))
                    nc.vector.tensor_reduce(neg_max[:, DQK + t:DQK + t + 1], scores[(t + 1) % 2][:, :], AX_X, ALU.max,
                                            negate=True).then_inc(row_max, 1)

                def transposed_half(i, c):
                    dve.wait_ge(xnT_done[i], nth(2, c, 2))
                    nc.vector.tensor_copy(tile4(xnT, 1), shared[1][:, :]).then_inc(xnT_b_ready[i], 1)

                def key_remainder(b, h):
                    dve.wait_ge(k_hi_ready, nth(2, b, h + 1))
                    nc.vector.scalar_tensor_tensor(k_l1[0:DQK, half(h)], scores[1][0:DQK, half(h)], bk_col[0:DQK, :],
                                                   k_hh[0:DQK, half(h)].bitcast(F32), ALU.add,
                                                   ALU.subtract).then_inc(k_ready, 1)

                def x1_half(a, h):
                    dve.wait_ge(den_rows_ready, nth(2, a, h + 1))
                    dve_attend.chain(dve, nc.vector.tensor_tensor(den_rows[:, half(h)], acc[:, half(h)], den_rows[:, half(h)], ALU.mult))
                    nc.vector.scalar_tensor_tensor(x1[:, half(h)], den_rows[:, half(h)], bv_col[:, :], x1[:, half(h)],
                                                   ALU.add, ALU.add).then_inc(x1_ready, 1)

                def y_remainder(c, h):
                    dve.wait_ge(y_hi_ready, nth(2, c, h + 1))
                    dve.wait_ge(ffn_done, nth(2, c - 1, 2))
                    nc.vector.tensor_tensor(tile4(y_lo, h), tile4(xnT, h), tile4(y_hi, h).bitcast(F32),
                                            ALU.subtract).then_inc(y_lo_ready, 1)

                def keys_turned(a, h):
                    dve.wait_ge(sc1_done, nth(1, a - 1, 1))
                    dve.wait_ge(kwT_done, nth(2, a, 2 - h))
                    nc.vector.tensor_tensor(kwT[:, 4 * h:4 * h + 4, :], shared[h][:, :].rearrange("p (t c) -> p t c", t=4),
                                            key_bias[:, 4 * h:4 * h + 4].unsqueeze(2).to_broadcast([P, 4, P]),
                                            ALU.add).then_inc(kwT_ready, 1)

                def half_of_x2(c, h):
                    dve.wait_ge(ffn_done, nth(2, c, h + 1))
                    dve.wait_ge(oscale_ready, nth(2, c, h + 1))
                    dve_chain.chain(dve, nc.vector.tensor_tensor(oscale[:, half(h)], shared[h][:, :], oscale[:, half(h)], ALU.mult))
                    nc.vector.tensor_tensor(res[:, half(h)], res[:, half(h)], oscale[:, half(h)], ALU.add).then_inc(x2_ready, 1)

                def body(k, prepare, attend, chain):
                    b, a, c = k, k - 1, k - 2
                    if chain:
                        dve_chain.begin(c)
                    if attend:
                        dve_attend.begin(a)
                        row_maximum(a, 0)
                    if chain:
                        dve.wait_ge(low_done, nth(1, c - 1, 1))
                        transposed_half(1, c)
                    if attend:
                        row_maximum(a, 1)
                        row_maximum(a, 2)
                    if chain:
                        dve.wait_ge(route_done, nth(1, c, 1))
                        nc.vector.tensor_reduce(r_max[0][:, :], shared[0][:, 0:E], AX_X, ALU.max,
                                                negate=True).then_inc(r_max_ready, 1)
                    if attend:
                        row_maximum(a, 3)
                    if chain:
                        dve.wait_ge(r_exp_ready, nth(1, c, 1))
                        dve_chain.chain(dve, nc.vector.reciprocal(r_inv[0][:, :], r_sum[0][:, :]))
                        dve_chain.chain(dve, nc.vector.tensor_scalar(route[:, :], r_exp[0][:, :], r_inv[0][:, :], None, ALU.mult))
                        dve.wait_ge(routeT_done, nth(1, c - 1, 1))
                        nc.vector.tensor_copy(route3[:, 0:E], route[:, :])
                        dve_chain.chain(dve, nc.vector.tensor_copy(route3[:, 64:64 + E], route[:, :]))
                        nc.vector.tensor_tensor(route3[:, 32:32 + E], route[:, :], route3[:, 0:E].bitcast(F32),
                                                ALU.subtract).then_inc(route_ready, 1)
                    if attend:
                        row_maximum(a, 4)
                        row_maximum(a, 5)
                    if chain:
                        for h in range(2):
                            dve.wait_ge(iscale_done, nth(2, c, h + 1))
                            nc.vector.tensor_tensor(tile4(xnT, h), tile4(xnT, h), shared[h][:, :], ALU.mult).then_inc(y_ready, 1)
                    if attend:
                        row_maximum(a, 6)
                    if chain:
                        y_remainder(c, 0)
                    if attend:
                        row_maximum(a, 7)
                    if chain:
                        y_remainder(c, 1)
                    if attend:
                        dve.wait_ge(max_turned, nth(1, a, 1))
                        for h in range(2):
                            nc.vector.tensor_tensor(
                                q_hm[DQK:DQK + T, half(h)].rearrange("r (t j) -> r t j", t=4),
                                scores[0][DQK:DQK + T, 0:P].unsqueeze(1).to_broadcast([T, 4, P]),
                                ident[DQK:DQK + T, DQK + 4 * h:DQK + 4 * h + 4].unsqueeze(2).to_broadcast([T, 4, P]),
                                ALU.mult).then_inc(max_ready, 1)
                    if chain:
                        dve.wait_ge(val_loaded, nth(16, c, 16))
                        dve.wait_ge(sc1_done, nth(1, c - 1, 1))
                        dve_chain.chain(dve, nc.vector.tensor_tensor_reduce(
                            out=unread[:, :], in0=c_val[:, :], in1=query_bias[:, :], scale=1.0, scalar=0.0,
                            op0=ALU.mult, op1=ALU.add, accum_out=key_sum[:, :]))
                        nc.vector.tensor_tensor(key_col[:, :], key_sum[:, :], bqbk[:, :], ALU.add).then_inc(key_col_ready, 1)
                        dve.wait_ge(biased, nth(1, c, 1))
                    for s in range(T):
                        if attend:
                            dve.wait_ge(p_hi_ready, nth(8, a, s + 1))
                            dve.wait_ge(pv_done, nth(8, a, s - 1))
                            nc.vector.tensor_tensor(p_lo[s % 2][:, :], prob[s % 2][:, :], p_hi[s % 2][:, :].bitcast(F32),
                                                    ALU.subtract).then_inc(p_lo_ready, 1)
                        if chain and s == 0:
                            half_of_x2(c, 0)
                        if chain and s == 1:
                            half_of_x2(c, 1)
                            dve.wait_ge(x2_ready, nth(2, c, 2))
                            statistics(dve_chain, 2, c, res)
                        if chain and s == 3:
                            transposed_half(2, c)
                        if prepare and s == 3:
                            dve.wait_ge(xn_loaded, nth(16, b, 16))
                            dve_prepare.begin(b)
                            statistics(dve_prepare, 0, b, xn)
                            dve_prepare.end()
                        if chain and s == 4:
                            dve.wait_ge(sc1_done, nth(1, c, 1))
                            nc.vector.tensor_reduce(r_max[1][:, :], shared[0][:, 0:P], AX_X, ALU.max,
                                                    negate=True).then_inc(s_max_ready, 1)
                        if attend and s in (4, 6):
                            keys_turned(a, (6 - s) // 2)
                        if prepare and s == 5:
                            dve.wait_ge(c_loaded, nth(16, b, 16))
                            dve.wait_ge(sc1_done, nth(1, c, 1))
                            nc.vector.tensor_copy(c_hi[:, :], c_in[:, :]).then_inc(c_hi_ready, 1)
                        if prepare and s == 6:
                            dve.wait_ge(c_hi_ready, nth(1, b, 1))
                            dve.wait_ge(xnT_done[2], nth(2, c, 2))
                            nc.vector.tensor_tensor(c_lo[:, :], c_in[:, :], c_hi[:, :].bitcast(F32),
                                                    ALU.subtract).then_inc(c_lo_ready, 1)
                        if chain and s == 6:
                            dve.wait_ge(attn_ready, nth(1, c, 1))
                            dve_chain.chain(dve, nc.vector.reciprocal(r_inv[1][:, :], r_sum[1][:, :]))
                    if chain:
                        for h in range(2):
                            dve.wait_ge(att_done, nth(2, c, h + 1))
                            nc.vector.scalar_tensor_tensor(res[:, half(h)], shared[h][:, :], r_inv[1][:, :], res[:, half(h)],
                                                           ALU.mult, ALU.add).then_inc(x3_ready, 1)
                    if chain:
                        dve.wait_ge(x3_ready, nth(2, c, 2))
                        statistics(dve_chain, 3, c, res)
                    if attend:
                        dve.wait_ge(den_done, nth(1, a, 1))
                        dve.wait_ge(den_turned, nth(2, a - 1, 2))
                        nc.vector.reciprocal(den_inv[:, :], scores[1][:, 0:T * T].rearrange("p (t e) -> p t e", t=T)[:, :, 0]
                                             ).then_inc(den_inv_ready, 1)
                    if prepare:
                        for h in range(2):
                            dve.wait_ge(q_hi_ready, nth(2, b, h + 1))
                            nc.vector.scalar_tensor_tensor(q_hl[DQK:P, half(h)], scores[0][DQK:P, half(h)], bq_col[DQK:P, :],
                                                           q_hl[DQK:P, half(h)].bitcast(F32), ALU.add,
                                                           ALU.subtract).then_inc(q_ready, 1)
                        dve.wait_ge(cT_hi_ready, nth(1, b, 1))
                        nc.vector.tensor_tensor(cT_lo[:, :, :].rearrange("p t c -> p (t c)"), shared[0][:, :],
                                                cT_hi[:, :, :].rearrange("p t c -> p (t c)").bitcast(F32),
                                                ALU.subtract).then_inc(cT_lo_ready, 1)
                    if attend:
                        dve.wait_ge(pv_done, nth(8, a, 8))
                        dve.wait_ge(x1_loaded, nth(16, a, 16))
                        x1_half(a, 0)
                    if chain:
                        transposed_half(3, c)
                    if attend:
                        x1_half(a, 1)
                    if attend:
                        dve.wait_ge(x1_ready, nth(2, a, 2))
                        statistics(dve_attend, 1, a, x1)
                        dve_attend.end()
                    if chain:
                        dve.wait_ge(low_done, nth(1, c, 1))
                        dve_chain.chain(dve, nc.vector.tensor_tensor(logit[:, :], shared[0][:, HR:HR + E], br_rows[:, :], ALU.add))
                        nc.vector.tensor_reduce(r_max[2][:, :], logit[:, :], AX_X, ALU.max, negate=True).then_inc(l_max_ready, 1)
                        dve.wait_ge(l_exp_ready, nth(1, c, 1))
                        dve_chain.chain(dve, nc.vector.reciprocal(r_inv[2][:, :], r_sum[2][:, :]))
                        dve_chain.chain(dve, nc.vector.tensor_scalar(route1[:, :], r_exp[1][:, :], r_inv[2][:, :], LORA, ALU.mult, ALU.mult))
                        dve.wait_ge(lowT_done, nth(1, c - 1, 1))
                        nc.vector.tensor_tensor(low[:, :].rearrange("p (h r) -> p h r", h=E),
                                                shared[0][:, 0:HR].rearrange("p (h r) -> p h r", h=E),
                                                route1[:, :].unsqueeze(2).to_broadcast([P, E, R]), ALU.mult).then_inc(low_ready, 1)
                    if prepare:
                        key_remainder(b, 0)
                    if chain:
                        dve.wait_ge(lowT_hi_ready, nth(1, c, 1))
                        dve.wait_ge(out_done, nth(2, c - 1, 2))
                        nc.vector.tensor_tensor(lowT_lo[:, :], shared[1][:, 0:P], lowT_hi[:, :].bitcast(F32),
                                                ALU.subtract).then_inc(lowT_lo_ready, 1)
                    if prepare:
                        key_remainder(b, 1)
                    if prepare:
                        for h in range(2):
                            dve.wait_ge(v_hi_ready, nth(2, b, h + 1))
                            nc.vector.tensor_tensor(tile4(v_lo, h), scores[0][:, half(h)], tile4(v_hi, h).bitcast(F32),
                                                    ALU.subtract).then_inc(v_ready, 1)
                    if chain:
                        dve.wait_ge(stored, nth(16, c - 1, 16))
                        for h in range(2):
                            dve.wait_ge(out_done, nth(2, c, h + 1))
                            nc.vector.tensor_tensor(result[:, half(h)], shared[h][:, :], res[:, half(h)], ALU.add).then_inc(out_ready, 1)
                        dve_chain.end()

                iterations(dve, body)

            @block.tensor
            def _(pe):
                mm = nc.tensor.matmul
                pe.wait_ge(const_made, 3)

                def transposes(h, src, semaphore):
                    for j in range(4):
                        t = 4 * h + j
                        last = nc.tensor.transpose(shared[h][:, j * P:(j + 1) * P], src[:, t * P:(t + 1) * P], ident[:, :])
                    last.then_inc(semaphore, 1)

                def project(to, h, w_hi, w_lo):
                    mm(to[:, half(h)], w_hi[:, :], c_hi[:, half(h)], start=True, stop=False)
                    mm(to[:, half(h)], w_hi[:, :], c_lo[:, half(h)], start=False, stop=False)
                    return mm(to[:, half(h)], w_lo[:, :], c_hi[:, half(h)], start=False, stop=True)

                def values(h):
                    for t in range(4 * h, 4 * h + 4):
                        last = mm(scores[0][:, t * P:(t + 1) * P], xn[:, t * P:(t + 1) * P], wvT[:, :], start=True, stop=True)
                    last.then_inc(v_done, 1)

                def query_scores(a, t):
                    if t == 0:
                        pe.wait_ge(q_ready, nth(2, a, 2))
                        pe.wait_ge(k_ready, nth(2, a, 2))
                    elif t == 1:
                        pe.wait_ge(v_ready, nth(2, a, 2))
                    else:
                        pe.wait_ge(row_max, nth(8, a, t - 1))
                    for h in range(2):
                        last = mm(scores[(t + 1) % 2][:, half(h)], q_hl[:, t * P:(t + 1) * P], k_hh[:, half(h)], start=True, stop=True)
                    last.then_inc(maxscores_done, 1)

                def keys_through_queries(a, units):
                    for u in units:
                        h, f = u // T, u % T
                        if u == 0:
                            pe.wait_ge(x1_ready, nth(2, a - 1, 2))
                            pe.wait_ge(cT_hi_ready, nth(1, a, 1))
                            pe.wait_ge(cT_lo_ready, nth(1, a, 1))
                            pe.wait_ge(cT_whole_ready, nth(1, a, 1))
                        if f < TS:
                            mm(acc[:, half(h)], cT_hi[:, f, :], m_hi[:, f, half(h)], start=f == 0, stop=False)
                            mm(acc[:, half(h)], cT_hi[:, f, :], m_lo[:, f, half(h)], start=False, stop=False)
                            last = mm(acc[:, half(h)], cT_lo[:, f, :], m_hi[:, f, half(h)], start=False, stop=f == T - 1)
                        else:
                            last = mm(acc[:, half(h)], cT_whole[:, f - TS, :], m_whole[:, f - TS, half(h)],
                                      start=f == 0, stop=f == T - 1)
                        if f == T - 1:
                            last.then_inc(kw_done, 1)

                def out_scale(c, h):
                    pe.wait_ge(y_ready, nth(2, c, h + 1))
                    mm(shared[h][:, :], route3T[:, :], ocs3[:, half(h)], start=True, stop=True).then_inc(oscale_done, 1)

                def feed_forward(h, fs):
                    for f in fs:
                        mm(shared[h][:, :], y_hi[:, f, :], signT[:, f, half(h)], start=f == 0, stop=False)
                        last = mm(shared[h][:, :], y_lo[:, f, :], signT[:, f, half(h)], start=False, stop=f == T - 1)
                    if f == T - 1:
                        last.then_inc(ffn_done, 1)

                def key_scores(a, s):
                    if s == 0:
                        pe.wait_ge(max_ready, nth(2, a, 2))
                    elif s == 1:
                        pe.wait_ge(row_max, nth(8, a, 7))
                    else:
                        pe.wait_ge(exp_ready, nth(8, a, s - 1))
                    for h in range(2):
                        mm(scores[s % 2][:, half(h)], k_hh[:, s * P:(s + 1) * P], q_hl[:, half(h)], start=True, stop=False)
                        last = mm(scores[s % 2][:, half(h)], k_l1[:, s * P:(s + 1) * P], q_hm[:, half(h)], start=False, stop=True)
                    last.then_inc(scores_done, 1)

                def weigh_values(a, s):
                    if s == 0:
                        pe.wait_ge(kw_ready, nth(2, a, 2))
                        pe.wait_ge(v_ready, nth(2, a, 2))
                    pe.wait_ge(p_hi_ready, nth(8, a, s + 1))
                    pe.wait_ge(p_lo_ready, nth(8, a, s + 1))
                    for v, p, first, end in ((v_hi, p_hi, s == 0, False), (v_lo, p_hi, False, False), (v_hi, p_lo, False, s == T - 1)):
                        for h in range(2):
                            last = mm(acc[:, half(h)], v[:, s, :], p[s % 2][:, half(h)], start=first, stop=end)
                    last.then_inc(pv_done, 1)

                def body(k, prepare, attend, chain):
                    b, a, c = k, k - 1, k - 2
                    for t in range(T):
                        if attend:
                            query_scores(a, t)
                        if chain and t == 1:
                            pe.wait_ge(normed[1], nth(1, c, 1))
                            for h in range(2):
                                pe.wait_ge(out_ready, nth(2, c - 1, h + 1))
                                transposes(h, xn_1, xnT_done[1])
                        if chain and t == 2:
                            pe.wait_ge(xnT_a_ready[1], nth(1, c, 1))
                            pe.wait_ge(xnT_b_ready[1], nth(1, c, 1))
                            for f in range(T):
                                last = mm(shared[0][:, 0:E], xnT[:, f, :], gateT[:, f, 0:E], start=f == 0, stop=f == T - 1)
                            last.then_inc(route_done, 1)
                        if chain and t == 4:
                            pe.wait_ge(route_ready, nth(1, c, 1))
                            nc.tensor.transpose(shared[1][0:96, 0:P], route3[:, :].bitcast(F32), ident[:, :]).then_inc(routeT_done, 1)
                        if chain and t == 5:
                            pe.wait_ge(routeT_ready, nth(1, c, 1))
                            pe.wait_ge(r_exp_ready, nth(1, c, 1))
                            for h in range(2):
                                for j in range(4):
                                    f = 4 * h + j
                                    last = mm(shared[h][:, j * P:(j + 1) * P], ics3[:, f * P:(f + 1) * P], route3T[:, :],
                                              start=True, stop=True)
                                last.then_inc(iscale_done, 1)
                        if chain and t == 6:
                            out_scale(c, 0)
                        if attend:
                            keys_through_queries(a, range(KW_UNITS[t], KW_UNITS[t + 1]))
                        if chain and t == 6:
                            out_scale(c, 1)
                    if attend:
                        pe.wait_ge(row_max, nth(8, a, 8))
                        nc.tensor.transpose(scores[0][0:DQK + T, 0:P], neg_max[:, 0:DQK + T], ident[:, :]).then_inc(max_turned, 1)
                    if chain:
                        pe.wait_ge(y_lo_ready, nth(2, c, 1))
                        pe.wait_ge(y_hi_ready, nth(2, c, 1))
                        pe.wait_ge(oscale_ready, nth(2, c, 1))
                        feed_forward(0, range(0, 4))
                    if attend:
                        key_scores(a, 0)
                        key_scores(a, 1)
                    if chain:
                        pe.wait_ge(y_lo_ready, nth(2, c, 2))
                        pe.wait_ge(y_hi_ready, nth(2, c, 2))
                        feed_forward(0, range(4, T))
                        pe.wait_ge(oscale_ready, nth(2, c, 2))
                        feed_forward(1, range(T))
                    for s in range(T):
                        if attend and s + 2 < T:
                            key_scores(a, s + 2)
                        if chain and s == 3:
                            pe.wait_ge(normed[2], nth(1, c, 1))
                            for h in range(2):
                                transposes(h, xn_2, xnT_done[2])
                        if chain and s == 4:
                            pe.wait_ge(xnT_a_ready[2], nth(1, c, 1))
                            pe.wait_ge(xnT_b_ready[2], nth(1, c, 1))
                            pe.wait_ge(kwT_ready, nth(2, c, 2))
                            pe.wait_ge(key_col_ready, nth(1, c, 1))
                            for f in range(T):
                                mm(shared[0][:, 0:P], xnT[:, f, :], kwT[:, f, :], start=f == 0, stop=False)
                            mm(shared[0][:, 0:P], key_col[:, :].to_broadcast([P, P]), ident[:, :], start=False,
                               stop=True).then_inc(sc1_done, 1)
                        if attend and s == 4:
                            transposes(1, kw, kwT_done)
                        if chain and s == 6:
                            pe.wait_ge(attn_ready, nth(1, c, 1))
                            pe.wait_ge(kwT_ready, nth(2, a, 1))
                            nc.tensor.transpose(shared[1][:, 0:P], attn[:, :], ident[:, :]).then_inc(attnT_done, 1)
                        if attend and s == 6:
                            transposes(0, kw, kwT_done)
                        if chain and s == 7:
                            pe.wait_ge(attnT_ready, nth(1, c, 1))
                            pe.wait_ge(kwT_ready, nth(2, a, 2))
                            pe.wait_ge(val_loaded, nth(16, c, 16))
                            for h in range(2):
                                mm(shared[h][:, :], attnT[:, :], c_val[:, half(h)], start=True, stop=True).then_inc(att_done, 1)
                        if prepare and s == 7:
                            pe.wait_ge(c_hi_ready, nth(1, b, 1))
                            pe.wait_ge(c_lo_ready, nth(1, b, 1))
                            pe.wait_ge(exp_ready, nth(8, a, 7))
                            for h in range(2):
                                project(scores[0], h, wqT_hi, wqT_lo).then_inc(q_done, 1)
                        if attend and s == 7:
                            pe.wait_ge(p_summed, nth(7, a, 7))
                            pe.wait_ge(exp_ready, nth(8, a, 8))
                            for t in range(T):
                                last = mm(scores[1][:, t * T:(t + 1) * T], p_sum[:, t * P:(t + 1) * P], ones[:, :], start=True, stop=True)
                            last.then_inc(den_done, 1)
                        if attend:
                            weigh_values(a, s)
                    if attend:
                        pe.wait_ge(den_inv_ready, nth(1, a, 1))
                        for h in range(2):
                            for j in range(4):
                                t = 4 * h + j
                                last = nc.tensor.transpose(scores[1][:, t * P:(t + 1) * P],
                                                           den_inv[:, t:t + 1].to_broadcast([P, P]), ident[:, :])
                            last.then_inc(den_turned, 1)
                    if prepare:
                        pe.wait_ge(c_loaded, nth(16, b, 16))
                        for h in range(2):
                            pe.wait_ge(x3_ready, nth(2, c, h + 1))
                            transposes(h, c_in, cT_done)
                        pe.wait_ge(den_rows_ready, nth(2, a, 2))
                        for h in range(2):
                            project(scores[1], h, wkT_hi, wkT_lo).then_inc(k_done, 1)
                    if chain:
                        pe.wait_ge(normed[3], nth(1, c, 1))
                        for h in range(2):
                            pe.wait_ge((cT_lo_ready, cT_whole_ready)[h], nth(1, b, 1))
                            transposes(h, xn_3, xnT_done[3])
                    if prepare:
                        pe.wait_ge(normed[0], nth(1, b, 1))
                        pe.wait_ge(q_ready, nth(2, b, 2))
                        values(0)
                        values(1)
                    if chain:
                        pe.wait_ge(xnT_a_ready[3], nth(1, c, 1))
                        pe.wait_ge(xnT_b_ready[3], nth(1, c, 1))
                        for f in range(T):
                            last = mm(shared[0][:, 0:HR + E], xnT[:, f, :], lowT[:, f, :], start=f == 0, stop=f == T - 1)
                        last.then_inc(low_done, 1)
                    if prepare:
                        keys_through_queries(b, range(0, 3))
                    if chain:
                        pe.wait_ge(low_ready, nth(1, c, 1))
                        nc.tensor.transpose(shared[1][:, 0:P], low[:, :], ident[:, :]).then_inc(lowT_done, 1)
                    if prepare:
                        keys_through_queries(b, range(3, KW_UNITS[0]))
                    if chain:
                        pe.wait_ge(lowT_hi_ready, nth(1, c, 1))
                        mm(shared[0][:, :], lowT_hi[:, :], bT_hi[:, half(0)], start=True, stop=False)
                        mm(shared[0][:, :], lowT_hi[:, :], bT_lo[:, half(0)], start=False, stop=False)
                        pe.wait_ge(lowT_lo_ready, nth(1, c, 1))
                        mm(shared[0][:, :], lowT_lo[:, :], bT_hi[:, half(0)], start=False, stop=True).then_inc(out_done, 1)
                        mm(shared[1][:, :], lowT_hi[:, :], bT_hi[:, half(1)], start=True, stop=False)
                        mm(shared[1][:, :], lowT_hi[:, :], bT_lo[:, half(1)], start=False, stop=False)
                        mm(shared[1][:, :], lowT_lo[:, :], bT_hi[:, half(1)], start=False, stop=True).then_inc(out_done, 1)

                iterations(pe, body)


_INS = ['x', 'ctx_4096', 'L0_xattn_Wq', 'L0_xattn_bq', 'L0_xattn_Wk', 'L0_xattn_bk', 'L0_xattn_Wv', 'L0_xattn_bv',
        'L0_ffn_weight', 'L0_ffn_bias', 'L0_ffn_gate_w', 'L0_ffn_in_channel_scale', 'L0_ffn_out_channel_scale',
        'L1_xattn_Wq', 'L1_xattn_bq', 'L1_xattn_Wk', 'L1_xattn_bk', 'L1_ffn_A', 'L1_ffn_B', 'L1_ffn_Wr', 'L1_ffn_br']


def kernel(**inputs):
    import numpy as np
    import concourse.bacc as bacc
    from concourse import mybir
    from concourse.bass_utils import run_bass_kernel_spmd

    nc = bacc.Bacc("TRN2", target_bir_lowering=False, num_devices=1)
    arrays, args = {}, []
    for name in _INS:
        a = np.ascontiguousarray(inputs[name])
        arrays[f"in_{name}"] = a
        args.append(nc.dram_tensor(f"in_{name}", a.shape, mybir.dt.from_np(a.dtype), kind="ExternalInput").ap())
    args.append(nc.dram_tensor("out_x", inputs["x"].shape, mybir.dt.float32, kind="ExternalOutput").ap())
    build(nc, *args)
    return run_bass_kernel_spmd(nc, [arrays], core_ids=[0]).results[0]["out_x"]
```
